# Optimizing a Trainium2 kernel written in Bass

```python
import numpy as np
import jax
import jax.numpy as jnp

def _softmax(x, axis=-1):
    return jax.nn.softmax(x, axis=axis)

def _gelu(x):
    return jax.nn.gelu(x, approximate=True)

def _silu(x):
    return jax.nn.silu(x)

def _sigmoid(x):
    return jax.nn.sigmoid(x)

def _layernorm(x, axis=-1, eps=1e-05):
    m = jnp.mean(x, axis=axis, keepdims=True)
    v = jnp.var(x, axis=axis, keepdims=True)
    return (x - m) / jnp.sqrt(v + eps)

def _scatter_add(tgt, idx, src, axis=0):
    return tgt.at[idx].add(src)

def _segment_sum(src, seg, n):
    return jax.ops.segment_sum(src, seg, n)
kernel_name = 'mk_recurrent_d1_jaxref_r8_3ba1ff'

def setup_inputs(seed: int=0):
    np.random.seed(seed)
    _w = jnp.asarray

    def _L0_attn_setup():
        import jax, jax.numpy as jnp
        import numpy as np
        B, S, D = (8, 256, 128)
        key = jax.random.key(seed)
        k1, k2, k3, k4 = jax.random.split(key, 4)
        return {'hidden_states': jax.random.normal(k1, (B, S, D), dtype=jnp.float32), 'w_dec_attn': jax.random.normal(k2, (D, D), dtype=jnp.float32), 'w_out': jax.random.normal(k3, (D, 2 * D), dtype=jnp.float32) * 0.02, 'b_out': jnp.zeros((D,), dtype=jnp.float32)}
    _L0_attn_in = _L0_attn_setup()

    def _L0_ffn_setup():
        import jax, jax.numpy as jnp
        import numpy as np
        DIM = 128
        DEPTH = 2
        HEADS = 8
        DIM_HEAD = 64
        WINDOW = 64
        INNER = HEADS * DIM_HEAD
        HID = int(DIM * 4 * 2 / 3)
        B, N = (2, 1024)
        QK_SCALE = 8.0

        def shift_token(t):
            t1, t2 = jnp.split(t, 2, axis=-1)
            t2 = jnp.pad(t2, ((0, 0), (1, 0), (0, 0)))[:, :-1]
            return jnp.concatenate([t1, t2], axis=-1)

        def l2norm(t):
            return t / jnp.clip(jnp.linalg.norm(t, axis=-1, keepdims=True), 1e-12)

        def rotate_half(x):
            x1, x2 = jnp.split(x, 2, axis=-1)
            return jnp.concatenate([-x2, x1], axis=-1)

        def rotary_xpos(q, k):
            n = q.shape[-2]
            half_idx = jnp.arange(0, DIM_HEAD, 2, dtype=jnp.float32)
            inv_freq = 1.0 / 10000.0 ** (half_idx / DIM_HEAD)
            t = jnp.arange(n, dtype=jnp.float32)
            freqs = t[:, None] * inv_freq[None, :]
            freqs = jnp.concatenate([freqs, freqs], axis=-1)
            base = (half_idx + 0.4 * DIM_HEAD) / (1.4 * DIM_HEAD)
            power = (t - n // 2) / float(WINDOW // 2)
            scale = base[None, :] ** power[:, None]
            scale = jnp.concatenate([scale, scale], axis=-1)
            cos, sin = (jnp.cos(freqs), jnp.sin(freqs))
            q = q * cos * scale + rotate_half(q) * sin * scale
            k = k * cos / scale + rotate_half(k) * sin / scale
            return (q, k)

        def local_attention(q, k, v):
            b, h, n, d = q.shape
            w = n // WINDOW
            bq = q.reshape(b, h, w, WINDOW, d) * QK_SCALE
            bk = k.reshape(b, h, w, WINDOW, d)
            bv = v.reshape(b, h, w, WINDOW, d)

            def look_around(t):
                p = jnp.pad(t, ((0, 0), (0, 0), (1, 0), (0, 0), (0, 0)))
                return jnp.concatenate([p[:, :, :w], p[:, :, 1:]], axis=3)
            bk, bv = (look_around(bk), look_around(bv))
            bt = jnp.arange(n).reshape(w, WINDOW)
            btp = jnp.pad(bt, ((1, 0), (0, 0)), constant_values=-1)
            btk = jnp.concatenate([btp[:w], btp[1:]], axis=1)
            sim = jnp.einsum('bhwid,bhwjd->bhwij', bq, bk)
            i = bt[:, :, None]
            j = btk[:, None, :]
            mask = (i < j) | (i > j + WINDOW) | (j == -1)
            sim = jnp.where(mask, -jnp.finfo(sim.dtype).max, sim)
            attn = jax.nn.softmax(sim, axis=-1)
            out = jnp.einsum('bhwij,bhwjd->bhwid', attn, bv)
            return out.reshape(b, h, n, d)

        def _layer(x, wqkv, qs, ksc, wo, lg, lb, w1, b1, w2, b2):
            b, n, _ = x.shape
            h = shift_token(x)
            qkv = h @ wqkv
            q, k, v = jnp.split(qkv, 3, axis=-1)
            to_heads = lambda t: t.reshape(b, n, HEADS, DIM_HEAD).transpose(0, 2, 1, 3)
            q, k, v = (to_heads(q), to_heads(k), to_heads(v))
            q = l2norm(q) * qs
            k = l2norm(k) * ksc
            q, k = rotary_xpos(q, k)
            o = local_attention(q, k, v)
            o = o.transpose(0, 2, 1, 3).reshape(b, n, INNER)
            x = x + o @ wo
            h = shift_token(x)
            mu = h.mean(-1, keepdims=True)
            var = h.var(-1, keepdims=True)
            h = (h - mu) / jnp.sqrt(var + 1e-05) * lg + lb
            h = h @ w1 + b1
            a, g = jnp.split(h, 2, axis=-1)
            h = a * jax.nn.gelu(g, approximate=False)
            x = x + h @ w2 + b2
            return x
        key = jax.random.key(seed)
        ks = jax.random.split(key, 6)
        return {'x': jax.random.normal(ks[0], (B, N, DIM), jnp.float32), 'wqkv': jax.random.normal(ks[1], (DEPTH, DIM, 3 * INNER), jnp.float32) * 0.02, 'q_scale': jnp.ones((DEPTH, DIM_HEAD), jnp.float32), 'k_scale': jnp.ones((DEPTH, DIM_HEAD), jnp.float32), 'wo': jax.random.normal(ks[2], (DEPTH, INNER, DIM), jnp.float32) * 0.02, 'ln_g': jnp.ones((DEPTH, DIM), jnp.float32), 'ln_b': jnp.zeros((DEPTH, DIM), jnp.float32), 'w1': jax.random.normal(ks[3], (DEPTH, DIM, 2 * HID), jnp.float32) * 0.02, 'b1': jnp.zeros((DEPTH, 2 * HID), jnp.float32), 'w2': jax.random.normal(ks[4], (DEPTH, HID, DIM), jnp.float32) * 0.02, 'b2': jnp.zeros((DEPTH, DIM), jnp.float32)}
    _L0_ffn_in = _L0_ffn_setup()
    _d = {'L0_attn_hidden_states': _L0_attn_in['hidden_states'], 'L0_attn_w_dec_attn': _L0_attn_in['w_dec_attn'], 'L0_attn_w_out': _L0_attn_in['w_out'], 'L0_attn_b_out': _L0_attn_in['b_out'], 'L0_ffn_wqkv': _L0_ffn_in['wqkv'], 'L0_ffn_q_scale': _L0_ffn_in['q_scale'], 'L0_ffn_k_scale': _L0_ffn_in['k_scale'], 'L0_ffn_wo': _L0_ffn_in['wo'], 'L0_ffn_ln_g': _L0_ffn_in['ln_g'], 'L0_ffn_ln_b': _L0_ffn_in['ln_b'], 'L0_ffn_w1': _L0_ffn_in['w1'], 'L0_ffn_b1': _L0_ffn_in['b1'], 'L0_ffn_w2': _L0_ffn_in['w2'], 'L0_ffn_b2': _L0_ffn_in['b2']}
    _x0 = _d['L0_attn_hidden_states']
    _d['L0_attn_hidden_states'] = jax.random.normal(jax.random.fold_in(jax.random.key(seed), 1), (16, 256, 128), dtype=_x0.dtype)
    del _x0
    return _d

def reference(L0_attn_hidden_states, L0_attn_w_dec_attn, L0_attn_w_out, L0_attn_b_out, L0_ffn_wqkv, L0_ffn_q_scale, L0_ffn_k_scale, L0_ffn_wo, L0_ffn_ln_g, L0_ffn_ln_b, L0_ffn_w1, L0_ffn_b1, L0_ffn_w2, L0_ffn_b2):

    def _L0_attn_ref(hidden_states, w_dec_attn, w_out, b_out):
        import jax, jax.numpy as jnp
        import numpy as np
        B, S, D = (8, 256, 128)
        b, s, d = hidden_states.shape
        q = hidden_states @ w_dec_attn
        scores = jnp.einsum('bid,bjd->bij', q, hidden_states)
        i_idx = jnp.arange(s)[:, None]
        j_idx = jnp.arange(s)[None, :]
        mask = j_idx < i_idx
        mask = mask.at[0, 0].set(True)
        attn = jax.nn.softmax(jnp.where(mask, scores, -jnp.inf), axis=-1)
        context = jnp.einsum('bij,bjd->bid', attn, hidden_states)
        combined = jnp.concatenate([hidden_states, context], axis=-1)
        out = jnp.tanh(combined @ w_out.T + b_out)
        return out

    def _L0_ffn_ref(x, wqkv, q_scale, k_scale, wo, ln_g, ln_b, w1, b1, w2, b2):
        import jax, jax.numpy as jnp
        import numpy as np
        DIM = 128
        DEPTH = 2
        HEADS = 8
        DIM_HEAD = 64
        WINDOW = 64
        INNER = HEADS * DIM_HEAD
        HID = int(DIM * 4 * 2 / 3)
        B, N = (2, 1024)
        QK_SCALE = 8.0

        def shift_token(t):
            t1, t2 = jnp.split(t, 2, axis=-1)
            t2 = jnp.pad(t2, ((0, 0), (1, 0), (0, 0)))[:, :-1]
            return jnp.concatenate([t1, t2], axis=-1)

        def l2norm(t):
            return t / jnp.clip(jnp.linalg.norm(t, axis=-1, keepdims=True), 1e-12)

        def rotate_half(x):
            x1, x2 = jnp.split(x, 2, axis=-1)
            return jnp.concatenate([-x2, x1], axis=-1)

        def rotary_xpos(q, k):
            n = q.shape[-2]
            half_idx = jnp.arange(0, DIM_HEAD, 2, dtype=jnp.float32)
            inv_freq = 1.0 / 10000.0 ** (half_idx / DIM_HEAD)
            t = jnp.arange(n, dtype=jnp.float32)
            freqs = t[:, None] * inv_freq[None, :]
            freqs = jnp.concatenate([freqs, freqs], axis=-1)
            base = (half_idx + 0.4 * DIM_HEAD) / (1.4 * DIM_HEAD)
            power = (t - n // 2) / float(WINDOW // 2)
            scale = base[None, :] ** power[:, None]
            scale = jnp.concatenate([scale, scale], axis=-1)
            cos, sin = (jnp.cos(freqs), jnp.sin(freqs))
            q = q * cos * scale + rotate_half(q) * sin * scale
            k = k * cos / scale + rotate_half(k) * sin / scale
            return (q, k)

        def local_attention(q, k, v):
            b, h, n, d = q.shape
            w = n // WINDOW
            bq = q.reshape(b, h, w, WINDOW, d) * QK_SCALE
            bk = k.reshape(b, h, w, WINDOW, d)
            bv = v.reshape(b, h, w, WINDOW, d)

            def look_around(t):
                p = jnp.pad(t, ((0, 0), (0, 0), (1, 0), (0, 0), (0, 0)))
                return jnp.concatenate([p[:, :, :w], p[:, :, 1:]], axis=3)
            bk, bv = (look_around(bk), look_around(bv))
            bt = jnp.arange(n).reshape(w, WINDOW)
            btp = jnp.pad(bt, ((1, 0), (0, 0)), constant_values=-1)
            btk = jnp.concatenate([btp[:w], btp[1:]], axis=1)
            sim = jnp.einsum('bhwid,bhwjd->bhwij', bq, bk)
            i = bt[:, :, None]
            j = btk[:, None, :]
            mask = (i < j) | (i > j + WINDOW) | (j == -1)
            sim = jnp.where(mask, -jnp.finfo(sim.dtype).max, sim)
            attn = jax.nn.softmax(sim, axis=-1)
            out = jnp.einsum('bhwij,bhwjd->bhwid', attn, bv)
            return out.reshape(b, h, n, d)

        def _layer(x, wqkv, qs, ksc, wo, lg, lb, w1, b1, w2, b2):
            b, n, _ = x.shape
            h = shift_token(x)
            qkv = h @ wqkv
            q, k, v = jnp.split(qkv, 3, axis=-1)
            to_heads = lambda t: t.reshape(b, n, HEADS, DIM_HEAD).transpose(0, 2, 1, 3)
            q, k, v = (to_heads(q), to_heads(k), to_heads(v))
            q = l2norm(q) * qs
            k = l2norm(k) * ksc
            q, k = rotary_xpos(q, k)
            o = local_attention(q, k, v)
            o = o.transpose(0, 2, 1, 3).reshape(b, n, INNER)
            x = x + o @ wo
            h = shift_token(x)
            mu = h.mean(-1, keepdims=True)
            var = h.var(-1, keepdims=True)
            h = (h - mu) / jnp.sqrt(var + 1e-05) * lg + lb
            h = h @ w1 + b1
            a, g = jnp.split(h, 2, axis=-1)
            h = a * jax.nn.gelu(g, approximate=False)
            x = x + h @ w2 + b2
            return x
        for l in range(DEPTH):
            x = _layer(x, wqkv[l], q_scale[l], k_scale[l], wo[l], ln_g[l], ln_b[l], w1[l], b1[l], w2[l], b2[l])
        return x
    x = L0_attn_hidden_states
    xn = _layernorm(x, axis=-1)
    s = _L0_attn_ref(xn, L0_attn_w_dec_attn, L0_attn_w_out, L0_attn_b_out)
    g = _silu(_L0_ffn_ref(xn, L0_ffn_wqkv, L0_ffn_q_scale, L0_ffn_k_scale, L0_ffn_wo, L0_ffn_ln_g, L0_ffn_ln_b, L0_ffn_w1, L0_ffn_b1, L0_ffn_w2, L0_ffn_b2))
    x = x + s * g
    return x

_drawn_inputs = setup_inputs


def setup_inputs(seed=0):
    import zlib

    import numpy as np

    out = dict(_drawn_inputs(seed))
    spreads = {'L0_attn_b_out': (0.0, 0.1),
     'L0_ffn_q_scale': (1.0, 0.6),
     'L0_ffn_k_scale': (1.0, 0.6),
     'L0_ffn_ln_g': (1.0, 0.6),
     'L0_ffn_ln_b': (0.0, 0.8),
     'L0_ffn_b1': (0.0, 0.8),
     'L0_ffn_b2': (0.0, 0.326)}
    factors = {'L0_ffn_wqkv': 8.0, 'L0_ffn_wo': 8.0, 'L0_ffn_w1': 8.0, 'L0_ffn_w2': 8.0}
    for name, (base, spread) in spreads.items():
        noise = np.random.default_rng([zlib.crc32(name.encode()), seed]).standard_normal(out[name].shape)
        drawn = base * np.exp(spread * noise) if base else spread * noise
        out[name] = jnp.asarray(drawn.astype(out[name].dtype))
    for name, factor in factors.items():
        out[name] = (out[name] * factor).astype(out[name].dtype)
    return out
```

```python
import numpy as np
import concourse.bass as bass
from concourse import mybir
from contextlib import ExitStack

F32 = mybir.dt.float32
BF16 = mybir.dt.bfloat16
ALU = mybir.AluOpType
ACT = mybir.ActivationFunctionType
AXX = mybir.AxisListType.X

P = 128
BATCH = 16
SEQ = 256
TPS = SEQ // P
NT = BATCH * TPS
D = 128
HALF = D // 2
LAYERS = 2
HEADS = 8
DH = 64
INNER = HEADS * DH
WIN = 64
NCH = INNER // P
HID = int(D * 4 * 2 / 3)
HC = 114
NHC = 3
HSIZE = [HC, HC, HID - 2 * HC]
EPS = 1e-5
MASKED = -(2.0 ** 126)
QK_SCALE = 8.0


def program(nc, x, w_dec, w_outT, b_out, wqkv, qk_scale, wo, ln_gb, w1, b1, w2, b2,
            rope, masks, identity, out):
    with ExitStack() as ctx:
        def sb(name, shape, dt=F32):
            return ctx.enter_context(nc.sbuf_tensor(name, shape, dt))

        def bank(name):
            return ctx.enter_context(nc.psum_tensor(name, [P, 512], F32))

        def sem(name):
            return ctx.enter_context(nc.semaphore(name))

        x_in = sb("x_in", [P, NT, D])
        x_res = sb("x_res", [P, NT, D])
        s_all = sb("s_all", [P, NT, D])
        h_shift = sb("h_shift", [P, NT, HALF])
        ident = sb("ident", [P, P])
        ident_bf = sb("ident_bf", [P, P], BF16)
        mask_f32 = sb("mask_f32", [P, 2 * 4 * P + 3 * P])
        mask_sb = sb("mask_sb", [P, 2 * 4 * P + 3 * P], BF16)
        win_mask = [mask_sb[:, t * 4 * P:(t + 1) * 4 * P] for t in range(TPS)]
        dec_mask = mask_sb[:, 8 * P:11 * P]
        rope_sb = sb("rope_sb", [P, 4, TPS, DH])
        rope_l = sb("rope_l", [P, 4, TPS, DH])
        qk_scale_sb = sb("qk_scale_sb", [P, LAYERS, 4, DH])
        w_dec_sb = sb("w_dec_sb", [P, D])
        w_out_sb = sb("w_out_sb", [P, 2, D])
        b_out_sb = sb("b_out_sb", [P, D])
        wqkv_sb = sb("wqkv_sb", [P, LAYERS, 3 * INNER])
        wo_sb = sb("wo_sb", [P, LAYERS, NCH, D])
        ln_sb = sb("ln_sb", [P, LAYERS, 2])
        w1_sb = sb("w1_sb", [P, 2 * HID])
        b1_sb = sb("b1_sb", [HC, LAYERS, 2 * NHC])
        ln_l = sb("ln_l", [P, 2])
        b1_l = sb("b1_l", [HC, 2 * NHC])
        w2_sb = sb("w2_sb", [HC, LAYERS, NHC, D])
        b2_sb = sb("b2_sb", [P, LAYERS, D])
        minus_half = sb("minus_half", [P, 2 * HEADS])
        stats = sb("stats", [P, TPS, 12])
        mean_var = sb("mean_var", [P, TPS, 2])
        var_eps = sb("var_eps", [P, TPS])
        rstd = sb("rstd", [P, TPS])
        xn = sb("xn", [P, TPS, D])
        xnT = sb("xnT", [P, SEQ])
        dq = sb("dq", [P, SEQ])
        d_nmax = sb("d_nmax", [P, TPS])
        d_den = sb("d_den", [P, TPS])
        d_rden = sb("d_rden", [P, TPS])
        dp = sb("dp", [P, 3 * P])
        dpT = sb("dpT", [P, 3 * P])
        dctx = sb("dctx", [P, TPS, D])
        dctxT = sb("dctxT", [P, SEQ])
        x_stage = sb("x_stage", [P, TPS, D])
        hT = sb("hT", [P, SEQ + 1])
        sq = sb("sq", [P, 2 * HEADS, DH])
        ssq = sb("ssq", [P, 2 * HEADS])
        ssq_c = sb("ssq_c", [P, 2 * HEADS])
        rnorm = sb("rnorm", [P, TPS, 2 * HEADS])
        qa = sb("qa", [P, INNER])
        qb = sb("qb", [P, INNER])
        qrot = sb("qrot", [P, INNER])
        khat = sb("khat", [P, INNER])
        ka = sb("ka", [P, INNER])
        kb = sb("kb", [P, INNER])
        krot = sb("krot", [P, INNER])
        qT = sb("qT", [P, NCH, P])
        kT = sb("kT", [P, NCH, SEQ])
        v_sb = sb("v_sb", [P, TPS, INNER])
        v_mid = sb("v_mid", [P, INNER])
        smax = sb("smax", [P, 2, 4])
        nbias = sb("nbias", [P, 2, 4])
        prob = sb("prob", [P, 2, 4 * P])
        den = sb("den", [P, 2, 4])
        rden = sb("rden", [P, 2, 4])
        pT = sb("pT", [P, 2, 4 * P])
        o_sb = sb("o_sb", [P, INNER])
        oT = sb("oT", [P, NCH, P])
        hn = sb("hn", [P, TPS, D])
        hnT = sb("hnT", [P, SEQ])
        gl = sb("gl", [HC, NHC, SEQ])
        hidT = sb("hidT", [HC, NHC, SEQ])
        gate = sb("gate", [P, 2, 4 * D])
        fin = sb("fin", [P, 2, 4 * D])

        B = [bank(f"bank{i}") for i in range(8)]

        seq_done = sem("seq_done")
        x_loaded = sem("x_loaded")
        const_loaded = sem("const_loaded")
        w1_loaded = sem("w1_loaded")
        const_made = sem("const_made")
        shifted = sem("shifted")
        aggregated = sem("aggregated")
        var_made = sem("var_made")
        rstd_made = sem("rstd_made")
        xn_ready = sem("xn_ready")
        xn_saved = sem("xn_saved")
        xnT_ready = sem("xnT_ready")
        xnT_copied = sem("xnT_copied")
        dq_ready = sem("dq_ready")
        dq_copied = sem("dq_copied")
        u_ready = sem("u_ready")
        u_saved = sem("u_saved")
        ds_ready = sem("ds_ready")
        dmax_ready = sem("dmax_ready")
        dp_ready = sem("dp_ready")
        drden_ready = sem("drden_ready")
        dpT_ready = sem("dpT_ready")
        dpT_copied = sem("dpT_copied")
        dctx_ready = sem("dctx_ready")
        dctx_scaled = sem("dctx_scaled")
        dctxT_ready = sem("dctxT_ready")
        dctxT_copied = sem("dctxT_copied")
        dout_ready = sem("dout_ready")
        tanh_done = sem("tanh_done")
        tables_ready = sem("tables_ready")
        x_staged = sem("x_staged")
        xT_ready = sem("xT_ready")
        hT_ready = sem("hT_ready")
        q_ready = sem("q_ready")
        k_ready = sem("k_ready")
        v_ready = sem("v_ready")
        sq_ready = sem("sq_ready")
        ssq_summed = sem("ssq_summed")
        ssq_ready = sem("ssq_ready")
        rnorm_ready = sem("rnorm_ready")
        qab_ready = sem("qab_ready")
        khat_ready = sem("khat_ready")
        kab_ready = sem("kab_ready")
        qrot_ready = sem("qrot_ready")
        krot_ready = sem("krot_ready")
        qT_ready = sem("qT_ready")
        qT_copied = sem("qT_copied")
        kT_ready = sem("kT_ready")
        kT_copied = sem("kT_copied")
        v_copied = sem("v_copied")
        vmid_ready = sem("vmid_ready")
        s_ready = sem("s_ready")
        smax_ready = sem("smax_ready")
        nbias_ready = sem("nbias_ready")
        p_ready = sem("p_ready")
        pTe_ready = sem("pTe_ready")
        pTe_copied = sem("pTe_copied")
        pTo_ready = sem("pTo_ready")
        pTo_copied = sem("pTo_copied")
        o_ready = sem("o_ready")
        rden_ready = sem("rden_ready")
        o_scaled = sem("o_scaled")
        oT_ready = sem("oT_ready")
        oT_copied = sem("oT_copied")
        y_ready = sem("y_ready")
        x_done = sem("x_done")
        hn_ready = sem("hn_ready")
        hnT_ready = sem("hnT_ready")
        hnT_copied = sem("hnT_copied")
        up_ready = sem("up_ready")
        gelu_ready = sem("gelu_ready")
        hid_ready = sem("hid_ready")
        b2_added = sem("b2_added")
        down_ready = sem("down_ready")
        silu_ready = sem("silu_ready")
        gated = sem("gated")
        fin_ready = sem("fin_ready")
        stored = [sem(f"stored{i}") for i in range(2)]

        N_CONST = 15

        def tile(buf, n):
            return buf[:, bass.ds(n, 1), :].rearrange("p a d -> p (a d)")

        def pair(buf, s):
            return buf[:, bass.ds(TPS * s, TPS), :]

        def heads(ap):
            return ap.rearrange("p (h e) -> p h e", e=DH)

        def later(count):
            return not (isinstance(count, int) and count == 0)

        def swapped(ap):
            return ap.rearrange("p (h k e) -> p h k e", k=2, e=DH // 2)[:, :, ::-1, :]

        def table(i, t):
            return rope_l[:, i, t, :].unsqueeze(1).broadcast_to([P, HEADS, DH])

        def table2(i, t):
            return rope_l[:, i, t, :].rearrange("p (k e) -> p k e", k=2).unsqueeze(1).broadcast_to(
                [P, HEADS, 2, DH // 2])

        block = ctx.enter_context(nc.Block())

        @block.sync
        def _(sp):
            sp.dma_start(x_in[:], x.rearrange("(n p) d -> p n d", p=P)).then_inc(x_loaded, 16)
            loads = [
                (ident[:], identity), (mask_f32[:], masks), (rope_sb[:], rope), (w_dec_sb[:], w_dec),
                (w_out_sb[:], w_outT), (b_out_sb[:], b_out.partition_broadcast(P)),
                (qk_scale_sb[:], qk_scale.partition_broadcast(P)),
                (wqkv_sb[:, 0, :], wqkv[0]), (wqkv_sb[:, 1, :], wqkv[1]), (wo_sb[:, 0], wo[0]), (wo_sb[:, 1], wo[1]),
                (ln_sb[:], ln_gb), (b1_sb[:], b1), (w2_sb[:], w2), (b2_sb[:], b2.partition_broadcast(P)),
            ]
            assert len(loads) == N_CONST
            for dst, src in loads:
                sp.dma_start(dst, src).then_inc(const_loaded, 16)
            with sp.Fori(0, LAYERS) as l:
                sp.wait_ge(seq_done, l * BATCH + BATCH)
                sp.dma_start(w1_sb[:], w1[bass.ds(l, 1)].rearrange("a p f -> (a p) f")).then_inc(w1_loaded, 16)
                with sp.Fori(0, BATCH) as s:
                    m = l * BATCH + s
                    sp.wait_ge(shifted, m * 32 + 32)
                    sp.wait_ge(x_done, m * TPS + TPS)
                    sp.dma_start(h_shift[1:P, bass.ds(TPS * s, TPS), :],
                                 x_res[0:P - 1, bass.ds(TPS * s, TPS), HALF:D]).then_inc(shifted, 16)
                    sp.dma_start(h_shift[0:1, bass.ds(TPS * s + 1, 1), :],
                                 x_res[P - 1:P, bass.ds(TPS * s, 1), HALF:D]).then_inc(shifted, 16)
            for c in range(NT // 4):
                sp.wait_ge(fin_ready, c + 1)
                sp.dma_start(out.rearrange("(n p) d -> p n d", p=P)[:, 4 * c:4 * c + 4, :],
                             fin[:, c % 2, :].rearrange("p (n d) -> p n d", n=4)).then_inc(stored[c % 2], 16)
            for i in range(2):
                sp.wait_ge(stored[i], 16 * (NT // 8))

        @block.gpsimd
        def _(pool):
            pool.wait_ge(const_made, 3)

            def inverse_std(i):
                pool.wait_ge(var_made, i + 1)
                pool.tensor_tensor(rstd[:], var_eps[:], minus_half[:, 0:TPS], ALU.pow).then_inc(rstd_made, 1)

            with pool.Fori(0, BATCH) as s:
                inverse_std(s)
                pool.wait_ge(xn_ready, s + 1)
                pool.tensor_copy(pair(x_res, s), xn[:]).then_inc(xn_saved, 1)

            def stage(s, t, n):
                pool.wait_ge(xT_ready, n - TPS + 1)
                pool.tensor_copy(x_stage[:, t, :], tile(x_res, TPS * s + t)).then_inc(x_staged, 1)

            def rope_sums(t, n, first=False):
                pool.wait_ge(ssq_ready, n + 1)
                pool.tensor_tensor(rnorm[:, t, :], ssq_c[:], minus_half[:], ALU.pow).then_inc(rnorm_ready, 1)
                pool.wait_ge(qab_ready, n + 1)
                if not first:
                    pool.wait_ge(qT_ready, n)
                pool.tensor_tensor(qrot[:], qa[:], qb[:], ALU.add).then_inc(qrot_ready, 1)
                pool.wait_ge(kab_ready, n + 1)
                if not first:
                    pool.wait_ge(kT_ready, n)
                pool.tensor_tensor(krot[:], ka[:], kb[:], ALU.add).then_inc(krot_ready, 1)

            with pool.Fori(0, LAYERS) as l:
                n0 = l * NT
                pool.wait_ge(seq_done, l * BATCH + BATCH)
                rope_sums(0, n0, first=True)

                def attend(s, last):
                    n = n0 + TPS * s
                    rope_sums(1, n + 1)
                    if not last:
                        stage(s + 1, 0, n + 2)
                        rope_sums(0, n + 2)
                        stage(s + 1, 1, n + 3)

                with pool.Fori(0, BATCH - 1) as s:
                    attend(s, False)
                attend(BATCH - 1, True)

                with pool.Fori(0, BATCH) as s:
                    m = l * BATCH + s
                    inverse_std(m + BATCH)
                    pool.wait_ge(hn_ready, m + 1)
                    pool.tensor_tensor(pair(x_res, s), pair(x_res, s),
                                       b2_sb[:, bass.ds(l, 1), :].broadcast_to([P, TPS, D]),
                                       ALU.add).then_inc(b2_added, 1)
            for c in range(NT // 4):
                g = gate[:, c % 2, :]
                pool.wait_ge(tanh_done, BATCH)
                pool.wait_ge(silu_ready, c + 1)
                pool.tensor_tensor(g, g, s_all[:, 4 * c:4 * c + 4, :].rearrange("p n d -> p (n d)"),
                                   ALU.mult).then_inc(gated, 1)

        @block.scalar
        def _(act):
            act.wait_ge(const_loaded, 16 * N_CONST)
            act.activation(mask_sb[:], mask_f32[:], ACT.Copy)
            act.activation(ident_bf[:], ident[:], ACT.Copy).then_inc(const_made, 1)

            def dec_transposed(s):
                act.wait_ge(xnT_ready, s + 1)
                act.activation(xnT[:], B[0][:, 0:SEQ], ACT.Copy).then_inc(xnT_copied, 1)
                act.wait_ge(dq_ready, s + 1)
                act.activation(dq[:], B[1][:, 0:SEQ], ACT.Copy).then_inc(dq_copied, 1)

            def dec_exp(s):
                act.wait_ge(dmax_ready, s + 1)
                for t in range(TPS):
                    a, b = t * P, t * P + (t + 1) * P
                    ins = act.activation(dp[:, a:b], B[2][:, a:b], ACT.Exp, bias=d_nmax[:, t:t + 1],
                                         accum_out=d_den[:, t:t + 1])
                ins.then_inc(dp_ready, 1)

            def dec_rest(s):
                act.wait_ge(dctxT_ready, s + 1)
                act.activation(dctxT[:], B[5][:, 0:SEQ], ACT.Copy).then_inc(dctxT_copied, 1)
                act.wait_ge(seq_done, s + 1)
                act.activation(pair(s_all, s), pair(s_all, s), ACT.Tanh).then_inc(tanh_done, 1)

            dec_transposed(0)
            with act.Fori(0, BATCH - 1) as s:
                dec_exp(s)
                dec_transposed(s + 1)
                dec_rest(s)
            dec_exp(BATCH - 1)
            dec_rest(BATCH - 1)

            def token_shift(t, n):
                act.wait_ge(xT_ready, n + 1)
                act.activation(hT[0:HALF, t * P:(t + 1) * P], B[5][0:HALF, 0:P], ACT.Copy)
                act.activation(hT[HALF:P, t * P + 1:(t + 1) * P + 1], B[5][HALF:P, 0:P],
                               ACT.Copy).then_inc(hT_ready, 1)

            def squares(n, first=False):
                if not first:
                    act.wait_ge(ssq_summed, n)
                act.wait_ge(k_ready, n + 1)
                act.activation(sq[:, HEADS:2 * HEADS, :], heads(B[1][:]), ACT.Square).then_inc(sq_ready, 1)
                act.wait_ge(q_ready, n + 1)
                act.activation(sq[:, 0:HEADS, :], heads(B[0][:]), ACT.Square).then_inc(sq_ready, 1)

            def values(t, n, vmid_count=None):
                act.wait_ge(v_ready, n + 1)
                if vmid_count is not None:
                    act.wait_ge(vmid_ready, vmid_count)
                act.activation(v_sb[:, t, :], B[2][:], ACT.Copy).then_inc(v_copied, 1)

            def q_transposed(n):
                act.wait_ge(qT_ready, n + 1)
                act.activation(qT[:].rearrange("p c n -> p (c n)"), B[6][:], ACT.Copy).then_inc(qT_copied, 1)

            def k_transposed(t, n):
                act.wait_ge(kT_ready, n + 1)
                act.activation(kT[:, :, t * P:(t + 1) * P], B[6][:].rearrange("p (c n) -> p c n", c=NCH),
                               ACT.Copy).then_inc(kT_copied, 1)

            def exps(t, n):
                for e in range(2):
                    act.wait_ge(nbias_ready, 2 * n + e + 1)
                    for j in range(4):
                        h = 2 * j + e
                        ins = act.activation(prob[:, e, j * P:(j + 1) * P], B[3 + e][:, j * P:(j + 1) * P], ACT.Exp,
                                             bias=nbias[:, e, j:j + 1], scale=rnorm[:, t, h:h + 1],
                                             accum_out=den[:, e, j:j + 1])
                    ins.then_inc(p_ready, 1)

            with act.Fori(0, LAYERS) as l:
                n0 = l * NT
                act.wait_ge(xn_saved, BATCH)
                act.wait_ge(seq_done, l * BATCH + BATCH)
                act.activation(x_stage[:], x_res[:, 0:TPS, :], ACT.Copy).then_inc(x_staged, TPS)
                token_shift(0, n0)
                squares(n0, first=True)
                values(0, n0)
                q_transposed(n0)
                k_transposed(0, n0)

                def attend(s, t, last):
                    n = n0 + TPS * s + t
                    if not last:
                        token_shift(1 - t, n + 1)
                    exps(t, n)
                    if not last:
                        squares(n + 1)
                    act.wait_ge(pTo_ready, n + 1)
                    act.activation(pT[:, 1, :], B[5][:], ACT.Copy).then_inc(pTo_copied, 1)
                    if not last:
                        values(1 - t, n + 1, l * BATCH + s + 1 if t else None)
                        q_transposed(n + 1)
                    act.wait_ge(oT_ready, n + 1)
                    act.activation(oT[:].rearrange("p c n -> p (c n)"), B[5][:], ACT.Copy).then_inc(oT_copied, 1)
                    if not last:
                        k_transposed(1 - t, n + 1)

                with act.Fori(0, BATCH - 1) as s:
                    attend(s, 0, False)
                    attend(s, 1, False)
                attend(BATCH - 1, 0, False)
                attend(BATCH - 1, 1, True)

                def normed(m):
                    act.wait_ge(hnT_ready, m + 1)
                    act.activation(hnT[:], B[6][:, 0:SEQ], ACT.Identity,
                                   scale=ln_l[:, 0:1], bias=ln_l[:, 1:2]).then_inc(hnT_copied, 1)

                def gelus(m):
                    for j in range(NHC):
                        act.wait_ge(up_ready, m * NHC + j + 1)
                        H = HSIZE[j]
                        act.activation(gl[0:H, j, :], B[j][0:H, SEQ:2 * SEQ], ACT.Gelu,
                                       bias=b1_l[0:H, NHC + j:NHC + j + 1]).then_inc(gelu_ready, 1)

                normed(l * BATCH)
                with act.Fori(0, BATCH - 1) as s:
                    gelus(l * BATCH + s)
                    normed(l * BATCH + s + 1)
                gelus(l * BATCH + BATCH - 1)

            act.wait_ge(seq_done, (LAYERS + 1) * BATCH)
            for c in range(NT // 4):
                if c >= 2:
                    act.wait_ge(fin_ready, c - 1)
                act.activation(gate[:, c % 2, :], x_res[:, 4 * c:4 * c + 4, :].rearrange("p n d -> p (n d)"),
                               ACT.Silu).then_inc(silu_ready, 1)

        @block.vector
        def _(dve):
            dve.memset(hT[HALF:P, 0:1], 0.0)
            dve.memset(h_shift[0:1, :, :], 0.0).then_inc(shifted, 32)
            dve.memset(minus_half[:], -0.5).then_inc(const_made, 2)
            dve.wait_ge(x_loaded, 16)
            dve.wait_ge(const_loaded, 16 * N_CONST)

            def norm_scale(dst, src, t, inc=None):
                ins = dve.tensor_scalar(dst, src, mean_var[:, t, 0:1], rstd[:, t:t + 1], ALU.subtract, ALU.mult)
                if inc is not None:
                    ins.then_inc(inc, 1)

            def dec_norm(s):
                for t in range(TPS):
                    ins = dve.bn_stats(stats[:, t, 0:6], tile(x_in, TPS * s + t))
                dve.drain()
                for t in range(TPS):
                    ins = dve.bn_aggr(mean_var[:, t, :], stats[:, t, 0:6])
                ins.then_inc(aggregated, 1)
                dve.wait_ge(aggregated, s + 1)
                dve.tensor_scalar(var_eps[:], mean_var[:, :, 1], EPS, None, ALU.add).then_inc(var_made, 1)
                dve.wait_ge(rstd_made, s + 1)
                if later(s):
                    dve.wait_ge(xnT_ready, s)
                    dve.wait_ge(xn_saved, s)
                norm_scale(xn[:, 0, :], tile(x_in, TPS * s), 0)
                norm_scale(xn[:, 1, :], tile(x_in, TPS * s + 1), 1, xn_ready)

            def dec_max(s):
                dve.wait_ge(u_ready, s + 1)
                dve.tensor_tensor(pair(s_all, s), B[6][:, 0:SEQ].rearrange("p (t d) -> p t d", t=TPS),
                                  b_out_sb[:].unsqueeze(1).broadcast_to([P, TPS, D]), ALU.add).then_inc(u_saved, 1)
                dve.wait_ge(ds_ready, s + 1)
                for t in range(TPS):
                    a, b = t * P, t * P + (t + 1) * P
                    ins = dve.tensor_reduce(d_nmax[:, t:t + 1], B[2][:, a:b], AXX, ALU.max, negate=True)
                ins.then_inc(dmax_ready, 1)

            def dec_rest(s):
                dve.wait_ge(dp_ready, s + 1)
                dve.reciprocal(d_rden[:], d_den[:]).then_inc(drden_ready, 1)
                dve.wait_ge(dpT_ready, s + 1)
                dve.tensor_copy(dpT[:], B[3][:, 0:3 * P]).then_inc(dpT_copied, 1)
                dve.wait_ge(drden_ready, s + 1)
                dve.wait_ge(dctx_ready, s + 1)
                for t in range(TPS):
                    ins = dve.tensor_scalar(dctx[:, t, :], B[4][:, t * D:(t + 1) * D], d_rden[:, t:t + 1], None,
                                            ALU.mult)
                ins.then_inc(dctx_scaled, 1)

            def dec_out(s):
                dve.wait_ge(u_saved, s + 1)
                dve.wait_ge(dout_ready, s + 1)
                dve.tensor_tensor(pair(s_all, s), B[7][:, 0:SEQ].rearrange("p (t d) -> p t d", t=TPS), pair(s_all, s),
                                  ALU.add).then_inc(seq_done, 1)

            dec_norm(0)
            dec_max(0)
            with dve.Fori(0, BATCH - 1) as s:
                dec_norm(s + 1)
                dec_rest(s)
                dec_max(s + 1)
                dec_out(s)
            dec_rest(BATCH - 1)
            dec_out(BATCH - 1)

            def sums(n, first=False):
                dve.wait_ge(sq_ready, 2 * n + 2)
                if not first:
                    dve.wait_ge(rnorm_ready, n)
                dve.tensor_reduce(ssq[:], sq[:], AXX, ALU.add).then_inc(ssq_summed, 1)
                dve.wait_ge(ssq_summed, n + 1)
                dve.tensor_scalar(ssq_c[:], ssq[:], 1e-24, None, ALU.max).then_inc(ssq_ready, 1)

            def rope_q(t, n, first=False):
                if not first:
                    dve.wait_ge(qrot_ready, n)
                dve.wait_ge(q_ready, n + 1)
                dve.tensor_tensor(heads(qa[:]), heads(B[0][:]), table(0, t), ALU.mult)
                dve.tensor_tensor(qb[:].rearrange("p (h k e) -> p h k e", k=2, e=DH // 2), swapped(B[0][:]),
                                  table2(1, t), ALU.mult).then_inc(qab_ready, 1)

            def rope_k(t, n, first=False):
                dve.wait_ge(rnorm_ready, n + 1)
                dve.wait_ge(k_ready, n + 1)
                dve.tensor_tensor(heads(khat[:]), heads(B[1][:]),
                                  rnorm[:, t, HEADS:2 * HEADS].unsqueeze(2).broadcast_to([P, HEADS, DH]),
                                  ALU.mult).then_inc(khat_ready, 1)
                dve.wait_ge(khat_ready, n + 1)
                if not first:
                    dve.wait_ge(krot_ready, n)
                dve.tensor_tensor(heads(ka[:]), heads(khat[:]), table(2, t), ALU.mult)
                dve.tensor_tensor(kb[:].rearrange("p (h k e) -> p h k e", k=2, e=DH // 2), swapped(khat[:]),
                                  table2(3, t), ALU.mult).then_inc(kab_ready, 1)

            def middle_values(n):
                dve.wait_ge(v_copied, n + 1)
                dve.tensor_copy(v_mid[0:WIN, :], v_sb[0:WIN, 1, :])
                dve.tensor_copy(v_mid[WIN:P, :], v_sb[WIN:P, 0, :]).then_inc(vmid_ready, 1)

            def maxima(t, n):
                for e in range(2):
                    dve.wait_ge(s_ready, 2 * n + e + 1)
                    dve.tensor_reduce(smax[:, e, :], B[3 + e][:].rearrange("p (j k) -> p j k", j=4), AXX,
                                      ALU.max).then_inc(smax_ready, 1)
                    dve.wait_ge(smax_ready, 2 * n + e + 1)
                    dve.scalar_tensor_tensor(out=nbias[:, e, :], in0=smax[:, e, :], scalar=-1.0,
                                             in1=rnorm[:, t, e:HEADS:2], op0=ALU.mult,
                                             op1=ALU.mult).then_inc(nbias_ready, 1)

            with dve.Fori(0, LAYERS) as l:
                n0 = l * NT
                dve.wait_ge(seq_done, l * BATCH + BATCH)
                for i in range(4):
                    dve.tensor_tensor(rope_l[:, i], rope_sb[:, i],
                                            qk_scale_sb[:, bass.ds(l, 1), i, :].broadcast_to([P, TPS, DH]), ALU.mult)
                dve.tensor_copy(ln_l[:], tile(ln_sb, l))
                dve.tensor_copy(b1_l[:], tile(b1_sb, l)).then_inc(tables_ready, 1)
                dve.wait_ge(tables_ready, l + 1)
                sums(n0, first=True)
                rope_q(0, n0, first=True)
                rope_k(0, n0, first=True)

                def attend(s, t, last):
                    n = n0 + TPS * s + t
                    maxima(t, n)
                    if t == 1:
                        middle_values(n)
                    dve.wait_ge(pTe_ready, n + 1)
                    dve.tensor_copy(pT[:, 0, :], B[6][:]).then_inc(pTe_copied, 1)
                    if not last:
                        sums(n + 1)
                        rope_q(1 - t, n + 1)
                    dve.wait_ge(p_ready, 2 * n + 2)
                    dve.reciprocal(rden[:], den[:]).then_inc(rden_ready, 1)
                    dve.wait_ge(rden_ready, n + 1)
                    dve.wait_ge(o_ready, n + 1)
                    dve.tensor_tensor(o_sb[:].rearrange("p (j e d) -> p j e d", e=2, d=DH),
                                      B[7][:].rearrange("p (j e d) -> p j e d", e=2, d=DH),
                                      rden[:].rearrange("p e j -> p j e").unsqueeze(3).broadcast_to([P, 4, 2, DH]),
                                      ALU.mult).then_inc(o_scaled, 1)
                    if not last:
                        rope_k(1 - t, n + 1)
                    dve.wait_ge(y_ready, n + 1)
                    xt = tile(x_res, TPS * s + t)
                    dve.tensor_tensor(xt, B[7][:, 0:D], xt, ALU.add).then_inc(x_done, 1)

                with dve.Fori(0, BATCH - 1) as s:
                    attend(s, 0, False)
                    attend(s, 1, False)
                attend(BATCH - 1, 0, False)
                attend(BATCH - 1, 1, True)

                def norm(s, m):
                    dve.wait_ge(shifted, 32 * m + 64)
                    dve.wait_ge(x_done, TPS * m + TPS)
                    for t in range(TPS):
                        dve.bn_stats(stats[:, t, 0:6], x_res[:, bass.ds(TPS * s + t, 1), 0:HALF].rearrange("p a d -> p (a d)"))
                        ins = dve.bn_stats(stats[:, t, 6:12], tile(h_shift, TPS * s + t))
                    dve.drain()
                    for t in range(TPS):
                        ins = dve.bn_aggr(mean_var[:, t, :], stats[:, t, :])
                    ins.then_inc(aggregated, 1)
                    dve.wait_ge(aggregated, BATCH + m + 1)
                    dve.tensor_scalar(var_eps[:], mean_var[:, :, 1], EPS, None, ALU.add).then_inc(var_made, 1)

                def norm_apply(s, m, first=False):
                    dve.wait_ge(rstd_made, BATCH + m + 1)
                    if not first:
                        dve.wait_ge(hnT_ready, m)
                    for t in range(TPS):
                        norm_scale(hn[:, t, 0:HALF],
                                   x_res[:, bass.ds(TPS * s + t, 1), 0:HALF].rearrange("p a d -> p (a d)"), t)
                        norm_scale(hn[:, t, HALF:D], tile(h_shift, TPS * s + t), t, hn_ready if t == TPS - 1 else None)

                def hidden(m):
                    for j in range(NHC):
                        H = HSIZE[j]
                        dve.wait_ge(gelu_ready, m * NHC + j + 1)
                        dve.scalar_tensor_tensor(out=hidT[0:H, j, :], in0=B[j][0:H, 0:SEQ],
                                                 scalar=b1_l[0:H, j:j + 1],
                                                 in1=gl[0:H, j, :], op0=ALU.add, op1=ALU.mult).then_inc(hid_ready, 1)

                def added(s, m):
                    dve.wait_ge(b2_added, m + 1)
                    dve.wait_ge(down_ready, m + 1)
                    xp = pair(x_res, s)
                    dve.tensor_tensor(xp, B[7][:, 0:SEQ].rearrange("p (t d) -> p t d", t=TPS), xp,
                                      ALU.add).then_inc(seq_done, 1)

                norm(0, l * BATCH)
                norm_apply(0, l * BATCH, first=True)
                with dve.Fori(0, BATCH - 1) as s:
                    m = l * BATCH + s
                    norm(s + 1, m + 1)
                    hidden(m)
                    norm_apply(s + 1, m + 1)
                    added(s, m)
                m = l * BATCH + BATCH - 1
                hidden(m)
                added(BATCH - 1, m)

            for c in range(NT // 4):
                dve.wait_ge(gated, c + 1)
                if c >= 2:
                    dve.wait_ge(stored[c % 2], 16 * (c // 2))
                dve.tensor_tensor(fin[:, c % 2, :], gate[:, c % 2, :],
                                  x_in[:, 4 * c:4 * c + 4, :].rearrange("p n d -> p (n d)"),
                                  ALU.add).then_inc(fin_ready, 1)

        @block.tensor
        def _(pe):
            pe.wait_ge(const_loaded, 16 * N_CONST)
            pe.wait_ge(const_made, 3)

            def dec_project(s):
                pe.wait_ge(xn_ready, s + 1)
                for t in range(TPS):
                    ins = pe.transpose(B[0][:, t * P:(t + 1) * P], xn[:, t, :], ident[:])
                ins.then_inc(xnT_ready, 1)
                pe.wait_ge(xnT_copied, s + 1)
                pe.matmul(B[1][:, 0:SEQ], w_dec_sb[:], xnT[:], start=True, stop=True).then_inc(dq_ready, 1)
                if later(s):
                    pe.wait_ge(u_saved, s)
                for t in range(TPS):
                    ins = pe.matmul(B[6][:, t * D:(t + 1) * D], xnT[:, t * P:(t + 1) * P], w_out_sb[:, 0, :],
                                    start=True, stop=True)
                ins.then_inc(u_ready, 1)

            def dec_scores(s):
                pe.wait_ge(dq_copied, s + 1)
                if later(s):
                    pe.wait_ge(dp_ready, s)
                pe.matmul(B[2][:, 0:3 * P], ident_bf[:], dec_mask, start=True, stop=False, skip_group_check=True)
                for t in range(TPS):
                    a, b = t * P, t * P + (t + 1) * P
                    ins = pe.matmul(B[2][:, a:b], dq[:, t * P:(t + 1) * P], xnT[:, 0:(t + 1) * P], start=False,
                                    stop=t == TPS - 1, skip_group_check=True)
                ins.then_inc(ds_ready, 1)

            def dec_context(s):
                pe.wait_ge(dp_ready, s + 1)
                for c in range(3):
                    ins = pe.transpose(B[3][:, c * P:(c + 1) * P], dp[:, c * P:(c + 1) * P], ident[:])
                ins.then_inc(dpT_ready, 1)
                pe.wait_ge(dpT_copied, s + 1)
                pe.wait_ge(xn_saved, s + 1)
                pe.matmul(B[4][:, 0:D], dpT[:, 0:P], tile(x_res, TPS * s), start=True, stop=True)
                pe.matmul(B[4][:, D:2 * D], dpT[:, P:2 * P], tile(x_res, TPS * s), start=True, stop=False)
                pe.matmul(B[4][:, D:2 * D], dpT[:, 2 * P:3 * P], tile(x_res, TPS * s + 1), start=False,
                          stop=True).then_inc(dctx_ready, 1)

            def dec_output(s):
                pe.wait_ge(dctx_scaled, s + 1)
                for t in range(TPS):
                    ins = pe.transpose(B[5][:, t * P:(t + 1) * P], dctx[:, t, :], ident[:])
                ins.then_inc(dctxT_ready, 1)
                pe.wait_ge(dctxT_copied, s + 1)
                if later(s):
                    pe.wait_ge(seq_done, s)
                for t in range(TPS):
                    ins = pe.matmul(B[7][:, t * D:(t + 1) * D], dctxT[:, t * P:(t + 1) * P], w_out_sb[:, 1, :],
                                    start=True, stop=True)
                ins.then_inc(dout_ready, 1)

            dec_project(0)
            dec_scores(0)
            with pe.Fori(0, BATCH - 1) as s:
                dec_project(s + 1)
                dec_context(s)
                dec_scores(s + 1)
                dec_output(s)
            dec_context(BATCH - 1)
            dec_output(BATCH - 1)

            def x_transpose(t, n):
                pe.wait_ge(x_staged, n + 1)
                pe.transpose(B[5][:, 0:P], x_stage[:, t, :], ident[:]).then_inc(xT_ready, 1)

            def project(l, t, n, first=False):
                pe.wait_ge(hT_ready, n + 1)
                lhs = hT[:, t * P:(t + 1) * P]

                def w(i):
                    return wqkv_sb[:, bass.ds(l, 1), i * INNER:(i + 1) * INNER].rearrange("p a f -> p (a f)")
                if not first:
                    pe.wait_ge(khat_ready, n)
                pe.matmul(B[1][:], lhs, w(1), start=True, stop=True).then_inc(k_ready, 1)
                if not first:
                    pe.wait_ge(qab_ready, n)
                pe.matmul(B[0][:], lhs, w(0), start=True, stop=True).then_inc(q_ready, 1)
                if not first:
                    pe.wait_ge(v_copied, n)
                pe.matmul(B[2][:], lhs, w(2), start=True, stop=True).then_inc(v_ready, 1)

            def transpose4(bank, src, inc):
                for c in range(4):
                    ins = pe.transpose(bank[:, c * P:(c + 1) * P], src[:, c * P:(c + 1) * P], ident[:])
                ins.then_inc(inc, 1)

            def q_transpose(n):
                pe.wait_ge(qrot_ready, n + 1)
                transpose4(B[6], qrot, qT_ready)

            def k_transpose(n):
                pe.wait_ge(krot_ready, n + 1)
                pe.wait_ge(qT_copied, n + 1)
                transpose4(B[6], krot, kT_ready)

            def scores(t, n):
                pe.wait_ge(kT_copied, n + 1)
                for e in range(2):
                    r = slice(e * DH, (e + 1) * DH)
                    S = B[3 + e]
                    pe.matmul(S[:], ident_bf[:], win_mask[t], start=True, stop=False, skip_group_check=True)
                    for j in range(4):
                        o = slice(j * P, (j + 1) * P)
                        if t == 0:
                            ins = pe.matmul(S[:, o], qT[r, j, :], kT[r, j, 0:P], start=False, stop=j == 3,
                                            skip_group_check=True)
                        else:
                            pe.matmul(S[0:WIN, o].rearrange("p (w k) -> p w k", w=2), qT[r, j, 0:WIN],
                                      kT[r, j, :].rearrange("p (w k) -> p w k", k=WIN)[:, 2:0:-1, :], start=False,
                                      stop=j == 3, skip_group_check=True)
                            ins = pe.matmul(S[WIN:P, o], qT[r, j, WIN:P], kT[r, j, P:2 * P], start=False, stop=j == 3,
                                            skip_group_check=True)
                    ins.then_inc(s_ready, 1)

            def apply_values(t, n, s_count):
                pe.wait_ge(p_ready, 2 * n + 1)
                transpose4(B[6], prob[:, 0, :], pTe_ready)
                pe.wait_ge(p_ready, 2 * n + 2)
                transpose4(B[5], prob[:, 1, :], pTo_ready)
                pe.wait_ge(v_copied, n + 1)
                if t:
                    pe.wait_ge(vmid_ready, s_count)
                for e in range(2):
                    pe.wait_ge((pTe_copied, pTo_copied)[e], n + 1)
                    for j in range(4):
                        h = slice((2 * j + e) * DH, (2 * j + e + 1) * DH)
                        if t == 0:
                            ins = pe.matmul(B[7][:, h], pT[:, e, j * P:(j + 1) * P], v_sb[:, 0, h], start=True,
                                            stop=True)
                        else:
                            pe.matmul(B[7][0:WIN, h], pT[:, e, j * P:j * P + WIN], v_mid[:, h], start=True, stop=True)
                            ins = pe.matmul(B[7][WIN:P, h], pT[:, e, j * P + WIN:(j + 1) * P], v_sb[:, 1, h],
                                            start=True, stop=True)
                ins.then_inc(o_ready, 1)

            def output(l, n):
                pe.wait_ge(oT_copied, n + 1)
                for c in range(NCH):
                    ins = pe.matmul(B[7][:, 0:D], oT[:, c, :],
                                    wo_sb[:, bass.ds(l, 1), c, :].rearrange("p a d -> p (a d)"), start=c == 0,
                                    stop=c == NCH - 1)
                ins.then_inc(y_ready, 1)

            with pe.Fori(0, LAYERS) as l:
                n0 = l * NT
                pe.wait_ge(seq_done, l * BATCH + BATCH)
                x_transpose(0, n0)
                project(l, 0, n0, first=True)
                q_transpose(n0)
                k_transpose(n0)

                def attend(s, t, last):
                    n = n0 + TPS * s + t
                    if not last:
                        x_transpose(1 - t, n + 1)
                    scores(t, n)
                    if not last:
                        project(l, 1 - t, n + 1)
                    apply_values(t, n, l * BATCH + s + 1)
                    if not last:
                        q_transpose(n + 1)
                    pe.wait_ge(o_scaled, n + 1)
                    transpose4(B[5], o_sb, oT_ready)
                    if not last:
                        k_transpose(n + 1)
                    output(l, n)

                with pe.Fori(0, BATCH - 1) as s:
                    attend(s, 0, False)
                    attend(s, 1, False)
                attend(BATCH - 1, 0, False)
                attend(BATCH - 1, 1, True)

                def hn_transpose(m):
                    pe.wait_ge(hn_ready, m + 1)
                    for t in range(TPS):
                        ins = pe.transpose(B[6][:, t * P:(t + 1) * P], hn[:, t, :], ident[:])
                    ins.then_inc(hnT_ready, 1)

                def up(m):
                    pe.wait_ge(hnT_copied, m + 1)
                    for j in range(NHC):
                        H = HSIZE[j]
                        pe.matmul(B[j][0:H, SEQ:2 * SEQ], w1_sb[:, HID + j * HC:HID + j * HC + H], hnT[:], start=True,
                                  stop=True)
                        pe.matmul(B[j][0:H, 0:SEQ], w1_sb[:, j * HC:j * HC + H], hnT[:], start=True,
                                  stop=True).then_inc(up_ready, 1)

                def down(m):
                    pe.wait_ge(seq_done, BATCH + m)
                    for t in range(TPS):
                        for j in range(NHC):
                            H = HSIZE[j]
                            pe.wait_ge(hid_ready, m * NHC + j + 1)
                            ins = pe.matmul(B[7][:, t * D:(t + 1) * D], hidT[0:H, j, t * P:(t + 1) * P],
                                            w2_sb[0:H, bass.ds(l, 1), j, :].rearrange("p a d -> p (a d)"),
                                            start=j == 0, stop=j == NHC - 1)
                    ins.then_inc(down_ready, 1)

                pe.wait_ge(w1_loaded, 16 * l + 16)
                pe.wait_ge(x_done, n0 + NT)
                hn_transpose(l * BATCH)
                with pe.Fori(0, BATCH - 1) as s:
                    up(l * BATCH + s)
                    hn_transpose(l * BATCH + s + 1)
                    down(l * BATCH + s)
                up(l * BATCH + BATCH - 1)
                down(l * BATCH + BATCH - 1)


def constants():
    a, b = np.arange(WIN)[:, None], np.arange(WIN)[None, :]
    causal, band, none = b <= a, b >= a, np.zeros((WIN, WIN), bool)
    first = np.block([[causal, none], [band, causal]])
    second = np.block([[causal, band], [band, causal]])
    i, j = np.arange(SEQ)[:, None], np.arange(SEQ)[None, :]
    dec = j < i
    dec[0, 0] = True
    seen = np.concatenate([first] * 4 + [second] * 4 + [dec[:P, :P], dec[P:, :]], axis=1)
    masks = np.where(seen, 0.0, MASKED).astype(np.float32)

    half_idx = np.arange(0, DH, 2, dtype=np.float32)
    inv_freq = (np.float32(1.0) / np.float32(10000.0) ** (half_idx / np.float32(DH))).astype(np.float32)
    tok = np.arange(SEQ, dtype=np.float32)
    freqs = tok[:, None] * inv_freq[None, :]
    freqs = np.concatenate([freqs, freqs], axis=-1)
    base = (half_idx + np.float32(0.4 * DH)) / np.float32(1.4 * DH)
    power = (tok - SEQ // 2) / np.float32(WIN // 2)
    scale = base[None, :] ** power[:, None]
    scale = np.concatenate([scale, scale], axis=-1)
    sign = np.where(np.arange(DH) < DH // 2, -1.0, 1.0).astype(np.float32)
    cos, sin = np.cos(freqs), np.sin(freqs) * sign
    tables = np.stack([QK_SCALE * cos * scale, QK_SCALE * sin * scale, cos / scale, sin / scale])
    rope = tables.reshape(4, TPS, P, DH).transpose(2, 0, 1, 3)
    return (np.ascontiguousarray(rope, dtype=np.float32), np.ascontiguousarray(masks),
            np.eye(P, dtype=np.float32))


def kernel(**inputs):
    import concourse.bacc as bacc
    from concourse.bass_utils import run_bass_kernel_spmd

    g = {k: np.asarray(v) for k, v in inputs.items()}
    w2 = np.zeros((LAYERS, NHC * HC, D), np.float32)
    w2[:, :HID] = g["L0_ffn_w2"]
    b1 = np.zeros((LAYERS, 2, NHC * HC), np.float32)
    b1[:, :, :HID] = g["L0_ffn_b1"].reshape(LAYERS, 2, HID)
    q_s, k_s = g["L0_ffn_q_scale"], g["L0_ffn_k_scale"]
    rope, masks, identity = constants()
    arrays = {
        "x": g["L0_attn_hidden_states"].reshape(BATCH * SEQ, D),
        "w_dec": g["L0_attn_w_dec_attn"],
        "w_outT": g["L0_attn_w_out"].T.reshape(2, D, D).transpose(1, 0, 2),
        "b_out": g["L0_attn_b_out"],
        "wqkv": g["L0_ffn_wqkv"],
        "qk_scale": np.stack([q_s, np.roll(q_s, DH // 2, -1), k_s, np.roll(k_s, DH // 2, -1)], axis=1),
        "wo": g["L0_ffn_wo"].reshape(LAYERS, NCH, P, D).transpose(0, 2, 1, 3),
        "ln_gb": np.stack([g["L0_ffn_ln_g"], g["L0_ffn_ln_b"]], axis=-1).transpose(1, 0, 2),
        "w1": g["L0_ffn_w1"],
        "b1": b1.reshape(LAYERS, 2 * NHC, HC).transpose(2, 0, 1),
        "w2": w2.reshape(LAYERS, NHC, HC, D).transpose(2, 0, 1, 3),
        "b2": g["L0_ffn_b2"],
        "rope": rope,
        "masks": masks,
        "identity": identity,
    }
    arrays = {f"in_{k}": np.ascontiguousarray(v) for k, v in arrays.items()}
    nc = bacc.Bacc("TRN2", target_bir_lowering=False, num_devices=1)
    aps = [nc.dram_tensor(k, v.shape, mybir.dt.from_np(v.dtype), kind="ExternalInput").ap() for k, v in arrays.items()]
    out = nc.dram_tensor("out", (BATCH * SEQ, D), F32, kind="ExternalOutput").ap()
    program(nc, *aps, out)
    r = run_bass_kernel_spmd(nc, [arrays], core_ids=[0])
    return r.results[0]["out"].reshape(BATCH, SEQ, D)
```

```python
import numpy as np
import concourse.bass as bass
from concourse import mybir
from contextlib import ExitStack

F32 = mybir.dt.float32
BF16 = mybir.dt.bfloat16
ALU = mybir.AluOpType
ACT = mybir.ActivationFunctionType
AXX = mybir.AxisListType.X

P = 128
BATCH = 16
SEQ = 256
TPS = SEQ // P
NT = BATCH * TPS
D = 128
HALF = D // 2
LAYERS = 2
HEADS = 8
DH = 64
INNER = HEADS * DH
WIN = 64
NCH = INNER // P
HID = int(D * 4 * 2 / 3)
HC = 114
NHC = 3
HSIZE = [HC, HC, HID - 2 * HC]
EPS = 1e-5
MASKED = -(2.0 ** 126)
QK_SCALE = 8.0


def program(nc, x, w_dec, w_outT, b_out, wqkv, qk_scale, wo, ln_gb, w1, b1, w2, b2,
            rope, masks, identity, out):
    with ExitStack() as ctx:
        def sb(name, shape, dt=F32):
            return ctx.enter_context(nc.sbuf_tensor(name, shape, dt))

        def sem(name):
            return ctx.enter_context(nc.semaphore(name))

        x_in = sb("x_in", [P, NT, D])
        x_res = sb("x_res", [P, NT, D])
        s_all = sb("s_all", [P, NT, D])
        h_shift = sb("h_shift", [P, NT, HALF])
        ident = sb("ident", [P, P])
        ident_bf = sb("ident_bf", [P, P], BF16)
        mask_f32 = sb("mask_f32", [P, 2 * 4 * P + 3 * P])
        mask_sb = sb("mask_sb", [P, 2 * 4 * P + 3 * P], BF16)
        win_mask = [mask_sb[:, t * 4 * P:(t + 1) * 4 * P] for t in range(TPS)]
        dec_mask = mask_sb[:, 8 * P:11 * P]
        rope_sb = sb("rope_sb", [P, 4, TPS, DH])
        rope_l = sb("rope_l", [P, 4, TPS, DH])
        qk_scale_sb = sb("qk_scale_sb", [P, LAYERS, 4, DH])
        w_dec_sb = sb("w_dec_sb", [P, D])
        w_out_sb = sb("w_out_sb", [P, 2, D])
        b_out_sb = sb("b_out_sb", [P, D])
        wqkv_sb = sb("wqkv_sb", [P, LAYERS, 3 * INNER])
        wo_sb = sb("wo_sb", [P, LAYERS, NCH, D])
        ln_sb = sb("ln_sb", [P, LAYERS, 2])
        w1_sb = sb("w1_sb", [P, 2 * HID])
        b1_sb = sb("b1_sb", [HC, LAYERS, 2 * NHC])
        ln_l = sb("ln_l", [P, 2])
        b1_l = sb("b1_l", [HC, 2 * NHC])
        w2_sb = sb("w2_sb", [HC, LAYERS, NHC, D])
        b2_sb = sb("b2_sb", [P, LAYERS, D])
        minus_half = sb("minus_half", [P, 2 * HEADS])
        stats = sb("stats", [P, TPS, 12])
        mean_var = sb("mean_var", [P, TPS, 2])
        var_eps = sb("var_eps", [P, TPS])
        rstd = sb("rstd", [P, TPS])
        xn = sb("xn", [P, TPS, D])
        xnT = sb("xnT", [P, SEQ])
        dq = sb("dq", [P, SEQ])
        d_nmax = sb("d_nmax", [P, TPS])
        d_den = sb("d_den", [P, TPS])
        d_rden = sb("d_rden", [P, TPS])
        dp = sb("dp", [P, 3 * P])
        dpT = sb("dpT", [P, 3 * P])
        dctx = sb("dctx", [P, TPS, D])
        dctxT = sb("dctxT", [P, SEQ])
        x_stage = sb("x_stage", [P, TPS, D])
        hT = sb("hT", [P, SEQ + 1])
        sq = sb("sq", [P, 2 * HEADS, DH])
        ssq = sb("ssq", [P, 2 * HEADS])
        ssq_c = sb("ssq_c", [P, 2 * HEADS])
        rnorm = sb("rnorm", [P, TPS, 2 * HEADS])
        qa = sb("qa", [P, INNER])
        qb = sb("qb", [P, INNER])
        qrot = sb("qrot", [P, INNER])
        khat = sb("khat", [P, INNER])
        ka = sb("ka", [P, INNER])
        kb = sb("kb", [P, INNER])
        krot = sb("krot", [P, INNER])
        qT = sb("qT", [P, NCH, P])
        kT = sb("kT", [P, NCH, SEQ])
        v_sb = sb("v_sb", [P, TPS, INNER])
        v_mid = sb("v_mid", [P, INNER])
        smax = sb("smax", [P, 2, 4])
        nbias = sb("nbias", [P, 2, 4])
        prob = sb("prob", [P, 2, 4 * P])
        den = sb("den", [P, 2, 4])
        rden = sb("rden", [P, 2, 4])
        pT = sb("pT", [P, 2, 4 * P])
        o_sb = sb("o_sb", [P, INNER])
        oT = sb("oT", [P, NCH, P])
        hn = sb("hn", [P, TPS, D])
        hnT = sb("hnT", [P, SEQ])
        gl = sb("gl", [HC, NHC, SEQ])
        hidT = sb("hidT", [HC, NHC, SEQ])
        gate = sb("gate", [P, 2, 4 * D])
        fin = sb("fin", [P, 2, 4 * D])

        psum = ctx.enter_context(nc.psum_tensor("psum", [P, 8, 512], F32))
        B = [psum[:, i, :] for i in range(8)]

        seq_done = sem("seq_done")
        x_loaded = sem("x_loaded")
        const_loaded = sem("const_loaded")
        w1_loaded = sem("w1_loaded")
        const_made = sem("const_made")
        shifted = sem("shifted")
        aggregated = sem("aggregated")
        var_made = sem("var_made")
        rstd_made = sem("rstd_made")
        xn_ready = sem("xn_ready")
        xn_saved = sem("xn_saved")
        xnT_ready = sem("xnT_ready")
        xnT_copied = sem("xnT_copied")
        dq_ready = sem("dq_ready")
        dq_copied = sem("dq_copied")
        u_ready = sem("u_ready")
        u_saved = sem("u_saved")
        ds_ready = sem("ds_ready")
        dmax_ready = sem("dmax_ready")
        dp_ready = sem("dp_ready")
        drden_ready = sem("drden_ready")
        dpT_ready = sem("dpT_ready")
        dpT_copied = sem("dpT_copied")
        dctx_ready = sem("dctx_ready")
        dctx_scaled = sem("dctx_scaled")
        dctxT_ready = sem("dctxT_ready")
        dctxT_copied = sem("dctxT_copied")
        dout_ready = sem("dout_ready")
        tanh_done = sem("tanh_done")
        tables_ready = sem("tables_ready")
        x_staged = sem("x_staged")
        xT_ready = sem("xT_ready")
        hT_ready = sem("hT_ready")
        q_ready = sem("q_ready")
        k_ready = sem("k_ready")
        v_ready = sem("v_ready")
        sq_ready = sem("sq_ready")
        ssq_summed = sem("ssq_summed")
        ssq_ready = sem("ssq_ready")
        rnorm_ready = sem("rnorm_ready")
        qab_ready = sem("qab_ready")
        khat_ready = sem("khat_ready")
        kab_ready = sem("kab_ready")
        qrot_ready = sem("qrot_ready")
        krot_ready = sem("krot_ready")
        qT_ready = sem("qT_ready")
        qT_copied = sem("qT_copied")
        kT_ready = sem("kT_ready")
        kT_copied = sem("kT_copied")
        v_copied = sem("v_copied")
        vmid_ready = sem("vmid_ready")
        s_ready = sem("s_ready")
        smax_ready = sem("smax_ready")
        nbias_ready = sem("nbias_ready")
        p_ready = sem("p_ready")
        pTe_ready = sem("pTe_ready")
        pTe_copied = sem("pTe_copied")
        pTo_ready = sem("pTo_ready")
        pTo_copied = sem("pTo_copied")
        o_ready = sem("o_ready")
        rden_ready = sem("rden_ready")
        o_scaled = sem("o_scaled")
        oT_ready = sem("oT_ready")
        oT_copied = sem("oT_copied")
        y_ready = sem("y_ready")
        x_done = sem("x_done")
        hn_ready = sem("hn_ready")
        hnT_ready = sem("hnT_ready")
        hnT_copied = sem("hnT_copied")
        up_ready = sem("up_ready")
        gelu_ready = sem("gelu_ready")
        hid_ready = sem("hid_ready")
        b2_added = sem("b2_added")
        down_ready = sem("down_ready")
        silu_ready = sem("silu_ready")
        gated = sem("gated")
        fin_ready = sem("fin_ready")
        stored = [sem(f"stored{i}") for i in range(2)]

        N_CONST = 15

        def tile(buf, n):
            return buf[:, bass.ds(n, 1), :].rearrange("p a d -> p (a d)")

        def pair(buf, s):
            return buf[:, bass.ds(TPS * s, TPS), :]

        def heads(ap):
            return ap.rearrange("p (h e) -> p h e", e=DH)

        def later(count):
            return not (isinstance(count, int) and count == 0)

        def swapped(ap):
            return ap.rearrange("p (h k e) -> p h k e", k=2, e=DH // 2)[:, :, ::-1, :]

        def table(i, t):
            return rope_l[:, i, t, :].unsqueeze(1).broadcast_to([P, HEADS, DH])

        def table2(i, t):
            return rope_l[:, i, t, :].rearrange("p (k e) -> p k e", k=2).unsqueeze(1).broadcast_to(
                [P, HEADS, 2, DH // 2])

        block = ctx.enter_context(nc.Block())

        @block.sync
        def _(sp):
            sp.dma_start(x_in[:], x.rearrange("(n p) d -> p n d", p=P)).then_inc(x_loaded, 16)
            loads = [
                (ident[:], identity), (mask_f32[:], masks), (rope_sb[:], rope), (w_dec_sb[:], w_dec),
                (w_out_sb[:], w_outT), (b_out_sb[:], b_out.partition_broadcast(P)),
                (qk_scale_sb[:], qk_scale.partition_broadcast(P)),
                (wqkv_sb[:, 0, :], wqkv[0]), (wqkv_sb[:, 1, :], wqkv[1]), (wo_sb[:, 0], wo[0]), (wo_sb[:, 1], wo[1]),
                (ln_sb[:], ln_gb), (b1_sb[:], b1), (w2_sb[:], w2), (b2_sb[:], b2.partition_broadcast(P)),
            ]
            assert len(loads) == N_CONST
            for dst, src in loads:
                sp.dma_start(dst, src).then_inc(const_loaded, 16)
            with sp.Fori(0, LAYERS) as l:
                sp.wait_ge(seq_done, l * BATCH + BATCH)
                sp.dma_start(w1_sb[:], w1[bass.ds(l, 1)].rearrange("a p f -> (a p) f")).then_inc(w1_loaded, 16)
                with sp.Fori(0, BATCH) as s:
                    m = l * BATCH + s
                    sp.wait_ge(shifted, m * 32 + 32)
                    sp.wait_ge(x_done, m * TPS + TPS)
                    sp.dma_start(h_shift[1:P, bass.ds(TPS * s, TPS), :],
                                 x_res[0:P - 1, bass.ds(TPS * s, TPS), HALF:D]).then_inc(shifted, 16)
                    sp.dma_start(h_shift[0:1, bass.ds(TPS * s + 1, 1), :],
                                 x_res[P - 1:P, bass.ds(TPS * s, 1), HALF:D]).then_inc(shifted, 16)
            for c in range(NT // 4):
                sp.wait_ge(fin_ready, c + 1)
                sp.dma_start(out.rearrange("(n p) d -> p n d", p=P)[:, 4 * c:4 * c + 4, :],
                             fin[:, c % 2, :].rearrange("p (n d) -> p n d", n=4)).then_inc(stored[c % 2], 16)
            for i in range(2):
                sp.wait_ge(stored[i], 16 * (NT // 8))

        @block.gpsimd
        def _(pool):
            pool.wait_ge(const_made, 3)

            def inverse_std(i):
                pool.wait_ge(var_made, i + 1)
                pool.tensor_tensor(rstd[:], var_eps[:], minus_half[:, 0:TPS], ALU.pow).then_inc(rstd_made, 1)

            with pool.Fori(0, BATCH) as s:
                inverse_std(s)
                pool.wait_ge(xn_ready, s + 1)
                pool.tensor_copy(pair(x_res, s), xn[:]).then_inc(xn_saved, 1)

            def inverse_norms(t, n):
                pool.wait_ge(ssq_ready, n + 1)
                pool.tensor_tensor(rnorm[:, t, :], ssq_c[:], minus_half[:], ALU.pow).then_inc(rnorm_ready, 1)

            def q_sum(n, first=False):
                pool.wait_ge(qab_ready, n + 1)
                if not first:
                    pool.wait_ge(qT_ready, n)
                pool.tensor_tensor(qrot[:], qa[:], qb[:], ALU.add).then_inc(qrot_ready, 1)

            def k_sum(n, first=False):
                pool.wait_ge(kab_ready, n + 1)
                if not first:
                    pool.wait_ge(kT_ready, n)
                pool.tensor_tensor(krot[:], ka[:], kb[:], ALU.add).then_inc(krot_ready, 1)

            with pool.Fori(0, LAYERS) as l:
                n0 = l * NT
                pool.wait_ge(seq_done, l * BATCH + BATCH)
                inverse_norms(0, n0)
                q_sum(n0, first=True)
                k_sum(n0, first=True)
                inverse_norms(1, n0 + 1)
                q_sum(n0 + 1)

                def attend(s, t, last):
                    n = n0 + TPS * s + t
                    if not (last and t):
                        k_sum(n + 1)
                    if not last:
                        inverse_norms(t, n + 2)
                        q_sum(n + 2)

                with pool.Fori(0, BATCH - 1) as s:
                    for t in range(TPS):
                        attend(s, t, False)
                for t in range(TPS):
                    attend(BATCH - 1, t, True)

                with pool.Fori(0, BATCH) as s:
                    m = l * BATCH + s
                    inverse_std(m + BATCH)
                    pool.wait_ge(hn_ready, m + 1)
                    pool.tensor_tensor(pair(x_res, s), pair(x_res, s),
                                       b2_sb[:, bass.ds(l, 1), :].broadcast_to([P, TPS, D]),
                                       ALU.add).then_inc(b2_added, 1)
            for c in range(NT // 4):
                g = gate[:, c % 2, :]
                pool.wait_ge(tanh_done, BATCH)
                pool.wait_ge(silu_ready, c + 1)
                pool.tensor_tensor(g, g, s_all[:, 4 * c:4 * c + 4, :].rearrange("p n d -> p (n d)"),
                                   ALU.mult).then_inc(gated, 1)

        @block.scalar
        def _(act):
            act.wait_ge(const_loaded, 16 * N_CONST)
            act.activation(mask_sb[:], mask_f32[:], ACT.Copy)
            act.activation(ident_bf[:], ident[:], ACT.Copy).then_inc(const_made, 1)

            def dec_transposed(s):
                act.wait_ge(xnT_ready, s + 1)
                act.activation(xnT[:], B[0][:, 0:SEQ], ACT.Copy).then_inc(xnT_copied, 1)
                act.wait_ge(dq_ready, s + 1)
                act.activation(dq[:], B[1][:, 0:SEQ], ACT.Copy).then_inc(dq_copied, 1)

            def dec_exp(s):
                act.wait_ge(dmax_ready, s + 1)
                for t in range(TPS):
                    a, b = t * P, t * P + (t + 1) * P
                    ins = act.activation(dp[:, a:b], B[2][:, a:b], ACT.Exp, bias=d_nmax[:, t:t + 1],
                                         accum_out=d_den[:, t:t + 1])
                ins.then_inc(dp_ready, 1)

            def dec_rest(s):
                act.wait_ge(dctxT_ready, s + 1)
                act.activation(dctxT[:], B[5][:, 0:SEQ], ACT.Copy).then_inc(dctxT_copied, 1)
                act.wait_ge(seq_done, s + 1)
                act.activation(pair(s_all, s), pair(s_all, s), ACT.Tanh).then_inc(tanh_done, 1)

            dec_transposed(0)
            with act.Fori(0, BATCH - 1) as s:
                dec_exp(s)
                dec_transposed(s + 1)
                dec_rest(s)
            dec_exp(BATCH - 1)
            dec_rest(BATCH - 1)

            def stage(s, t, n):
                act.wait_ge(xT_ready, n - TPS + 1)
                act.activation(x_stage[:, t, :], tile(x_res, TPS * s + t), ACT.Copy).then_inc(x_staged, 1)

            def token_shift(t, n):
                act.wait_ge(xT_ready, n + 1)
                act.activation(hT[0:HALF, t * P:(t + 1) * P], B[5][0:HALF, 0:P], ACT.Copy)
                act.activation(hT[HALF:P, t * P + 1:(t + 1) * P + 1], B[5][HALF:P, 0:P],
                               ACT.Copy).then_inc(hT_ready, 1)

            def squares(n, first=False):
                if not first:
                    act.wait_ge(ssq_summed, n)
                act.wait_ge(q_ready, n + 1)
                act.activation(sq[:, 0:HEADS, :], heads(B[0]), ACT.Square).then_inc(sq_ready, 1)
                act.wait_ge(k_ready, n + 1)
                act.activation(sq[:, HEADS:2 * HEADS, :], heads(B[1]), ACT.Square).then_inc(sq_ready, 1)

            def values(t, n, vmid_count=None):
                act.wait_ge(v_ready, n + 1)
                if vmid_count is not None:
                    act.wait_ge(vmid_ready, vmid_count)
                act.activation(v_sb[:, t, :], B[2], ACT.Copy).then_inc(v_copied, 1)

            def q_transposed(n):
                act.wait_ge(qT_ready, n + 1)
                act.activation(qT[:].rearrange("p c n -> p (c n)"), B[6], ACT.Copy).then_inc(qT_copied, 1)

            def k_transposed(t, n):
                act.wait_ge(kT_ready, n + 1)
                act.activation(kT[:, :, t * P:(t + 1) * P], B[6].rearrange("p (c n) -> p c n", c=NCH),
                               ACT.Copy).then_inc(kT_copied, 1)

            def exps(t, n):
                for e in range(2):
                    act.wait_ge(nbias_ready, 2 * n + e + 1)
                    for j in range(4):
                        h = 2 * j + e
                        ins = act.activation(prob[:, e, j * P:(j + 1) * P], B[3 + e][:, j * P:(j + 1) * P], ACT.Exp,
                                             bias=nbias[:, e, j:j + 1], scale=rnorm[:, t, h:h + 1],
                                             accum_out=den[:, e, j:j + 1])
                    ins.then_inc(p_ready, 1)

            with act.Fori(0, LAYERS) as l:
                n0 = l * NT
                act.wait_ge(xn_saved, BATCH)
                act.wait_ge(seq_done, l * BATCH + BATCH)
                act.activation(x_stage[:], x_res[:, 0:TPS, :], ACT.Copy).then_inc(x_staged, TPS)
                token_shift(0, n0)
                squares(n0, first=True)
                values(0, n0)
                token_shift(1, n0 + 1)
                q_transposed(n0)
                k_transposed(0, n0)
                squares(n0 + 1)
                values(1, n0 + 1)

                def attend(s, t, last):
                    n = n0 + TPS * s + t
                    if not last:
                        stage(s + 1, t, n + 2)
                        token_shift(t, n + 2)
                    exps(t, n)
                    act.wait_ge(pTo_ready, n + 1)
                    act.activation(pT[:, 1, :], B[5], ACT.Copy).then_inc(pTo_copied, 1)
                    if not last:
                        squares(n + 2)
                    if not (last and t):
                        q_transposed(n + 1)
                    if not last:
                        values(t, n + 2, l * BATCH + s + 1 if t == 0 else None)
                    act.wait_ge(oT_ready, n + 1)
                    act.activation(oT[:].rearrange("p c n -> p (c n)"), B[5], ACT.Copy).then_inc(oT_copied, 1)
                    if not (last and t):
                        k_transposed(1 - t, n + 1)

                with act.Fori(0, BATCH - 1) as s:
                    for t in range(TPS):
                        attend(s, t, False)
                for t in range(TPS):
                    attend(BATCH - 1, t, True)

                def gelus(m):
                    for j in range(NHC):
                        act.wait_ge(up_ready, m * NHC + j + 1)
                        H = HSIZE[j]
                        act.activation(gl[0:H, j, :], B[j][0:H, SEQ:2 * SEQ], ACT.Gelu,
                                       bias=b1_l[0:H, NHC + j:NHC + j + 1]).then_inc(gelu_ready, 1)

                gelus(l * BATCH)
                with act.Fori(1, BATCH) as s:
                    gelus(l * BATCH + s)

            act.wait_ge(seq_done, (LAYERS + 1) * BATCH)
            for c in range(NT // 4):
                if c >= 2:
                    act.wait_ge(fin_ready, c - 1)
                act.activation(gate[:, c % 2, :], x_res[:, 4 * c:4 * c + 4, :].rearrange("p n d -> p (n d)"),
                               ACT.Silu).then_inc(silu_ready, 1)

        @block.vector
        def _(dve):
            dve.memset(hT[HALF:P, 0:1], 0.0)
            dve.memset(h_shift[0:1, :, :], 0.0).then_inc(shifted, 32)
            dve.memset(minus_half[:], -0.5).then_inc(const_made, 2)
            dve.wait_ge(x_loaded, 16)
            dve.wait_ge(const_loaded, 16 * N_CONST)

            def norm_scale(dst, src, t, inc=None):
                ins = dve.tensor_scalar(dst, src, mean_var[:, t, 0:1], rstd[:, t:t + 1], ALU.subtract, ALU.mult)
                if inc is not None:
                    ins.then_inc(inc, 1)

            def dec_stats(s):
                for t in range(TPS):
                    ins = dve.bn_stats(stats[:, t, 0:6], tile(x_in, TPS * s + t))
                dve.drain()
                for t in range(TPS):
                    ins = dve.bn_aggr(mean_var[:, t, :], stats[:, t, 0:6])
                ins.then_inc(aggregated, 1)
                dve.wait_ge(aggregated, s + 1)
                dve.tensor_scalar(var_eps[:], mean_var[:, :, 1], EPS, None, ALU.add).then_inc(var_made, 1)

            def dec_norm(s):
                dve.wait_ge(rstd_made, s + 1)
                if later(s):
                    dve.wait_ge(xnT_ready, s)
                    dve.wait_ge(xn_saved, s)
                norm_scale(xn[:, 0, :], tile(x_in, TPS * s), 0)
                norm_scale(xn[:, 1, :], tile(x_in, TPS * s + 1), 1, xn_ready)

            def dec_saves(s):
                dve.wait_ge(u_ready, s + 1)
                dve.tensor_tensor(pair(s_all, s), B[6][:, 0:SEQ].rearrange("p (t d) -> p t d", t=TPS),
                                  b_out_sb[:].unsqueeze(1).broadcast_to([P, TPS, D]), ALU.add).then_inc(u_saved, 1)

            def dec_max(s):
                dve.wait_ge(ds_ready, s + 1)
                for t in range(TPS):
                    a, b = t * P, t * P + (t + 1) * P
                    ins = dve.tensor_reduce(d_nmax[:, t:t + 1], B[2][:, a:b], AXX, ALU.max, negate=True)
                ins.then_inc(dmax_ready, 1)

            def dec_rest(s, ahead):
                dve.wait_ge(dp_ready, s + 1)
                dve.reciprocal(d_rden[:], d_den[:]).then_inc(drden_ready, 1)
                dve.wait_ge(dpT_ready, s + 1)
                dve.tensor_copy(dpT[:], B[3][:, 0:3 * P]).then_inc(dpT_copied, 1)
                dve.wait_ge(drden_ready, s + 1)
                dve.wait_ge(dctx_ready, s + 1)
                for t in range(TPS):
                    ins = dve.tensor_scalar(dctx[:, t, :], B[4][:, t * D:(t + 1) * D], d_rden[:, t:t + 1], None,
                                            ALU.mult)
                ins.then_inc(dctx_scaled, 1)
                if ahead:
                    dec_saves(s + 1)

            def dec_out(s):
                dve.wait_ge(u_saved, s + 1)
                dve.wait_ge(dout_ready, s + 1)
                dve.tensor_tensor(pair(s_all, s), B[7][:, 0:SEQ].rearrange("p (t d) -> p t d", t=TPS), pair(s_all, s),
                                  ALU.add).then_inc(seq_done, 1)

            dec_stats(0)
            dec_norm(0)
            dec_stats(1)
            dec_saves(0)
            dec_max(0)
            dec_norm(1)
            dec_stats(2)

            def dec_turn(s, ahead):
                dec_rest(s, ahead)
                if ahead:
                    dec_max(s + 1)
                dec_out(s)
                if ahead > 1:
                    dec_norm(s + 2)
                if ahead > 2:
                    dec_stats(s + 3)

            with dve.Fori(0, BATCH - 3) as s:
                dec_turn(s, 3)
            for s in range(BATCH - 3, BATCH):
                dec_turn(s, BATCH - 1 - s)

            def sums(n, first=False):
                dve.wait_ge(sq_ready, 2 * n + 2)
                if not first:
                    dve.wait_ge(rnorm_ready, n)
                dve.tensor_reduce(ssq[:], sq[:], AXX, ALU.add).then_inc(ssq_summed, 1)
                dve.wait_ge(ssq_summed, n + 1)
                dve.tensor_scalar(ssq_c[:], ssq[:], 1e-24, None, ALU.max).then_inc(ssq_ready, 1)

            def rope_q(t, n, first=False):
                if not first:
                    dve.wait_ge(qrot_ready, n)
                dve.wait_ge(q_ready, n + 1)
                dve.tensor_tensor(heads(qa[:]), heads(B[0]), table(0, t), ALU.mult)
                dve.tensor_tensor(qb[:].rearrange("p (h k e) -> p h k e", k=2, e=DH // 2), swapped(B[0]),
                                  table2(1, t), ALU.mult).then_inc(qab_ready, 1)

            def rope_k(t, n, first=False):
                dve.wait_ge(rnorm_ready, n + 1)
                dve.wait_ge(k_ready, n + 1)
                dve.tensor_tensor(heads(khat[:]), heads(B[1]),
                                  rnorm[:, t, HEADS:2 * HEADS].unsqueeze(2).broadcast_to([P, HEADS, DH]),
                                  ALU.mult).then_inc(khat_ready, 1)
                dve.wait_ge(khat_ready, n + 1)
                if not first:
                    dve.wait_ge(krot_ready, n)
                dve.tensor_tensor(heads(ka[:]), heads(khat[:]), table(2, t), ALU.mult)
                dve.tensor_tensor(kb[:].rearrange("p (h k e) -> p h k e", k=2, e=DH // 2), swapped(khat[:]),
                                  table2(3, t), ALU.mult).then_inc(kab_ready, 1)

            def middle_values(n):
                dve.wait_ge(v_copied, n + 1)
                dve.tensor_copy(v_mid[0:WIN, :], v_sb[0:WIN, 1, :])
                dve.tensor_copy(v_mid[WIN:P, :], v_sb[WIN:P, 0, :]).then_inc(vmid_ready, 1)

            def maxima(t, n):
                for e in range(2):
                    dve.wait_ge(s_ready, 2 * n + e + 1)
                    dve.tensor_reduce(smax[:, e, :], B[3 + e].rearrange("p (j k) -> p j k", j=4), AXX,
                                      ALU.max).then_inc(smax_ready, 1)
                    dve.wait_ge(smax_ready, 2 * n + e + 1)
                    dve.scalar_tensor_tensor(out=nbias[:, e, :], in0=smax[:, e, :], scalar=-1.0,
                                             in1=rnorm[:, t, e:HEADS:2], op0=ALU.mult,
                                             op1=ALU.mult).then_inc(nbias_ready, 1)

            with dve.Fori(0, LAYERS) as l:
                n0 = l * NT
                dve.wait_ge(seq_done, l * BATCH + BATCH)
                for i in range(4):
                    dve.tensor_tensor(rope_l[:, i], rope_sb[:, i],
                                            qk_scale_sb[:, bass.ds(l, 1), i, :].broadcast_to([P, TPS, DH]), ALU.mult)
                dve.tensor_copy(ln_l[:], tile(ln_sb, l))
                dve.tensor_copy(b1_l[:], tile(b1_sb, l)).then_inc(tables_ready, 1)
                dve.wait_ge(tables_ready, l + 1)
                sums(n0, first=True)
                rope_q(0, n0, first=True)
                rope_k(0, n0, first=True)
                sums(n0 + 1)
                rope_q(1, n0 + 1)

                def attend(s, t, last):
                    n = n0 + TPS * s + t
                    maxima(t, n)
                    if not (last and t):
                        rope_k(1 - t, n + 1)
                    if t == 0:
                        middle_values(n + 1)
                    dve.wait_ge(pTe_ready, n + 1)
                    dve.tensor_copy(pT[:, 0, :], B[6]).then_inc(pTe_copied, 1)
                    dve.wait_ge(p_ready, 2 * n + 2)
                    dve.reciprocal(rden[:], den[:]).then_inc(rden_ready, 1)
                    dve.wait_ge(rden_ready, n + 1)
                    dve.wait_ge(o_ready, n + 1)
                    dve.tensor_tensor(o_sb[:].rearrange("p (j e d) -> p j e d", e=2, d=DH),
                                      B[7].rearrange("p (j e d) -> p j e d", e=2, d=DH),
                                      rden[:].rearrange("p e j -> p j e").unsqueeze(3).broadcast_to([P, 4, 2, DH]),
                                      ALU.mult).then_inc(o_scaled, 1)
                    if not last:
                        sums(n + 2)
                        rope_q(t, n + 2)
                    dve.wait_ge(y_ready, n + 1)
                    xt = tile(x_res, TPS * s + t)
                    dve.tensor_tensor(xt, B[7][:, 0:D], xt, ALU.add).then_inc(x_done, 1)

                with dve.Fori(0, BATCH - 1) as s:
                    for t in range(TPS):
                        attend(s, t, False)
                for t in range(TPS):
                    attend(BATCH - 1, t, True)

                def norm(s, m):
                    dve.wait_ge(shifted, 32 * m + 64)
                    dve.wait_ge(x_done, TPS * m + TPS)
                    for t in range(TPS):
                        dve.bn_stats(stats[:, t, 0:6], x_res[:, bass.ds(TPS * s + t, 1), 0:HALF].rearrange("p a d -> p (a d)"))
                        ins = dve.bn_stats(stats[:, t, 6:12], tile(h_shift, TPS * s + t))
                    dve.drain()
                    for t in range(TPS):
                        ins = dve.bn_aggr(mean_var[:, t, :], stats[:, t, :])
                    ins.then_inc(aggregated, 1)
                    dve.wait_ge(aggregated, BATCH + m + 1)
                    dve.tensor_scalar(var_eps[:], mean_var[:, :, 1], EPS, None, ALU.add).then_inc(var_made, 1)

                def norm_apply(s, m, first=False):
                    dve.wait_ge(rstd_made, BATCH + m + 1)
                    if not first:
                        dve.wait_ge(hnT_ready, m)
                    for t in range(TPS):
                        norm_scale(hn[:, t, 0:HALF],
                                   x_res[:, bass.ds(TPS * s + t, 1), 0:HALF].rearrange("p a d -> p (a d)"), t)
                        norm_scale(hn[:, t, HALF:D], tile(h_shift, TPS * s + t), t, hn_ready if t == TPS - 1 else None)

                def normed(m):
                    dve.wait_ge(hnT_ready, m + 1)
                    dve.tensor_scalar(hnT[:], B[6][:, 0:SEQ], ln_l[:, 0:1], ln_l[:, 1:2], ALU.mult,
                                      ALU.add).then_inc(hnT_copied, 1)

                def hidden(m):
                    for j in range(NHC):
                        H = HSIZE[j]
                        dve.wait_ge(gelu_ready, m * NHC + j + 1)
                        dve.scalar_tensor_tensor(out=hidT[0:H, j, :], in0=B[j][0:H, 0:SEQ],
                                                 scalar=b1_l[0:H, j:j + 1],
                                                 in1=gl[0:H, j, :], op0=ALU.add, op1=ALU.mult).then_inc(hid_ready, 1)

                def added(s, m):
                    dve.wait_ge(b2_added, m + 1)
                    dve.wait_ge(down_ready, m + 1)
                    xp = pair(x_res, s)
                    dve.tensor_tensor(xp, psum[:, 3:5, 0:D], xp, ALU.add).then_inc(seq_done, 1)

                norm(0, l * BATCH)
                norm_apply(0, l * BATCH, first=True)
                norm(1, l * BATCH + 1)
                normed(l * BATCH)

                def turn(s, ahead):
                    m = l * BATCH + s
                    if ahead > 0:
                        norm_apply(s + 1, m + 1)
                    hidden(m)
                    if ahead > 0:
                        normed(m + 1)
                    if ahead > 1:
                        norm(s + 2, m + 2)
                    added(s, m)

                with dve.Fori(0, BATCH - 2) as s:
                    turn(s, 2)
                turn(BATCH - 2, 1)
                turn(BATCH - 1, 0)

            for c in range(NT // 4):
                dve.wait_ge(gated, c + 1)
                if c >= 2:
                    dve.wait_ge(stored[c % 2], 16 * (c // 2))
                dve.tensor_tensor(fin[:, c % 2, :], gate[:, c % 2, :],
                                  x_in[:, 4 * c:4 * c + 4, :].rearrange("p n d -> p (n d)"),
                                  ALU.add).then_inc(fin_ready, 1)

        @block.tensor
        def _(pe):
            pe.wait_ge(const_loaded, 16 * N_CONST)
            pe.wait_ge(const_made, 3)

            def dec_transpose(s):
                pe.wait_ge(xn_ready, s + 1)
                for t in range(TPS):
                    ins = pe.transpose(B[0][:, t * P:(t + 1) * P], xn[:, t, :], ident[:])
                ins.then_inc(xnT_ready, 1)

            def dec_project(s):
                pe.wait_ge(xnT_copied, s + 1)
                pe.matmul(B[1][:, 0:SEQ], w_dec_sb[:], xnT[:], start=True, stop=True).then_inc(dq_ready, 1)
                if later(s):
                    pe.wait_ge(u_saved, s)
                for t in range(TPS):
                    ins = pe.matmul(B[6][:, t * D:(t + 1) * D], xnT[:, t * P:(t + 1) * P], w_out_sb[:, 0, :],
                                    start=True, stop=True)
                ins.then_inc(u_ready, 1)

            def dec_scores(s):
                pe.wait_ge(dq_copied, s + 1)
                if later(s):
                    pe.wait_ge(dp_ready, s)
                pe.matmul(B[2][:, 0:3 * P], ident_bf[:], dec_mask, start=True, stop=False, skip_group_check=True)
                for t in range(TPS):
                    a, b = t * P, t * P + (t + 1) * P
                    ins = pe.matmul(B[2][:, a:b], dq[:, t * P:(t + 1) * P], xnT[:, 0:(t + 1) * P], start=False,
                                    stop=t == TPS - 1, skip_group_check=True)
                ins.then_inc(ds_ready, 1)

            def dec_p_transpose(s):
                pe.wait_ge(dp_ready, s + 1)
                for c in range(3):
                    ins = pe.transpose(B[3][:, c * P:(c + 1) * P], dp[:, c * P:(c + 1) * P], ident[:])
                ins.then_inc(dpT_ready, 1)

            def dec_context(s):
                pe.wait_ge(dpT_copied, s + 1)
                pe.wait_ge(xn_saved, s + 1)
                pe.matmul(B[4][:, 0:D], dpT[:, 0:P], tile(x_res, TPS * s), start=True, stop=True)
                pe.matmul(B[4][:, D:2 * D], dpT[:, P:2 * P], tile(x_res, TPS * s), start=True, stop=False)
                pe.matmul(B[4][:, D:2 * D], dpT[:, 2 * P:3 * P], tile(x_res, TPS * s + 1), start=False,
                          stop=True).then_inc(dctx_ready, 1)

            def dec_c_transpose(s):
                pe.wait_ge(dctx_scaled, s + 1)
                for t in range(TPS):
                    ins = pe.transpose(B[5][:, t * P:(t + 1) * P], dctx[:, t, :], ident[:])
                ins.then_inc(dctxT_ready, 1)

            def dec_output(s):
                pe.wait_ge(dctxT_copied, s + 1)
                if later(s):
                    pe.wait_ge(seq_done, s)
                for t in range(TPS):
                    ins = pe.matmul(B[7][:, t * D:(t + 1) * D], dctxT[:, t * P:(t + 1) * P], w_out_sb[:, 1, :],
                                    start=True, stop=True)
                ins.then_inc(dout_ready, 1)

            dec_transpose(0)
            dec_project(0)
            dec_scores(0)

            def dec_turn(s, last):
                if not last:
                    dec_transpose(s + 1)
                dec_p_transpose(s)
                if not last:
                    dec_project(s + 1)
                dec_context(s)
                if not last:
                    dec_scores(s + 1)
                dec_c_transpose(s)
                dec_output(s)

            with pe.Fori(0, BATCH - 1) as s:
                dec_turn(s, False)
            dec_turn(BATCH - 1, True)

            def x_transpose(t, n):
                pe.wait_ge(x_staged, n + 1)
                pe.transpose(B[5][:, 0:P], x_stage[:, t, :], ident[:]).then_inc(xT_ready, 1)

            def project(l, t, i, bank_free, ready, n, first=False):
                if not first:
                    pe.wait_ge(bank_free, n)
                pe.matmul(B[i], hT[:, t * P:(t + 1) * P],
                          wqkv_sb[:, bass.ds(l, 1), i * INNER:(i + 1) * INNER].rearrange("p a f -> p (a f)"),
                          start=True, stop=True).then_inc(ready, 1)

            def project_qk(l, t, n, first=False):
                pe.wait_ge(hT_ready, n + 1)
                project(l, t, 0, qab_ready, q_ready, n, first)
                project(l, t, 1, khat_ready, k_ready, n, first)

            def project_v(l, t, n, first=False):
                project(l, t, 2, v_copied, v_ready, n, first)

            def transpose4(bank, src, inc):
                for c in range(4):
                    ins = pe.transpose(bank[:, c * P:(c + 1) * P], src[:, c * P:(c + 1) * P], ident[:])
                ins.then_inc(inc, 1)

            def q_transpose(n):
                pe.wait_ge(qrot_ready, n + 1)
                transpose4(B[6], qrot, qT_ready)

            def k_transpose(n):
                pe.wait_ge(krot_ready, n + 1)
                pe.wait_ge(qT_copied, n + 1)
                transpose4(B[6], krot, kT_ready)

            def scores(t, n, e):
                pe.wait_ge(kT_copied, n + 1)
                r = slice(e * DH, (e + 1) * DH)
                S = B[3 + e]
                pe.matmul(S, ident_bf[:], win_mask[t], start=True, stop=False, skip_group_check=True)
                for j in range(4):
                    o = slice(j * P, (j + 1) * P)
                    if t == 0:
                        ins = pe.matmul(S[:, o], qT[r, j, :], kT[r, j, 0:P], start=False, stop=j == 3,
                                        skip_group_check=True)
                    else:
                        pe.matmul(S[0:WIN, o].rearrange("p (w k) -> p w k", w=2), qT[r, j, 0:WIN],
                                  kT[r, j, :].rearrange("p (w k) -> p w k", k=WIN)[:, 2:0:-1, :], start=False,
                                  stop=j == 3, skip_group_check=True)
                        ins = pe.matmul(S[WIN:P, o], qT[r, j, WIN:P], kT[r, j, P:2 * P], start=False, stop=j == 3,
                                        skip_group_check=True)
                ins.then_inc(s_ready, 1)

            def apply_values(t, n, s_count):
                pe.wait_ge(p_ready, 2 * n + 1)
                transpose4(B[6], prob[:, 0, :], pTe_ready)
                pe.wait_ge(p_ready, 2 * n + 2)
                transpose4(B[5], prob[:, 1, :], pTo_ready)
                pe.wait_ge(v_copied, n + 1)
                if t:
                    pe.wait_ge(vmid_ready, s_count)
                for e in range(2):
                    pe.wait_ge((pTe_copied, pTo_copied)[e], n + 1)
                    for j in range(4):
                        h = slice((2 * j + e) * DH, (2 * j + e + 1) * DH)
                        pe.matmul(B[7][0:WIN, h], pT[:, e, j * P:j * P + WIN], (v_mid if t else v_sb[:, 0, :])[:, h],
                                  start=True, stop=True)
                        ins = pe.matmul(B[7][WIN:P, h], pT[:, e, j * P + WIN:(j + 1) * P], v_sb[:, t, h],
                                        start=True, stop=True)
                ins.then_inc(o_ready, 1)

            def output(l, n):
                pe.wait_ge(oT_copied, n + 1)
                for c in range(NCH):
                    ins = pe.matmul(B[7][:, 0:D], oT[:, c, :],
                                    wo_sb[:, bass.ds(l, 1), c, :].rearrange("p a d -> p (a d)"), start=c == 0,
                                    stop=c == NCH - 1)
                ins.then_inc(y_ready, 1)

            with pe.Fori(0, LAYERS) as l:
                n0 = l * NT
                pe.wait_ge(seq_done, l * BATCH + BATCH)
                x_transpose(0, n0)
                project_qk(l, 0, n0, first=True)
                project_v(l, 0, n0, first=True)
                x_transpose(1, n0 + 1)
                q_transpose(n0)
                k_transpose(n0)
                project_qk(l, 1, n0 + 1)
                project_v(l, 1, n0 + 1)

                def attend(s, t, last):
                    n = n0 + TPS * s + t
                    scores(t, n, 0)
                    if not last:
                        x_transpose(t, n + 2)
                    scores(t, n, 1)
                    if not last:
                        project_qk(l, t, n + 2)
                    apply_values(t, n, l * BATCH + s + 1)
                    if not (last and t):
                        q_transpose(n + 1)
                    if not last:
                        project_v(l, t, n + 2)
                    pe.wait_ge(o_scaled, n + 1)
                    transpose4(B[5], o_sb, oT_ready)
                    if not (last and t):
                        k_transpose(n + 1)
                    output(l, n)

                with pe.Fori(0, BATCH - 1) as s:
                    for t in range(TPS):
                        attend(s, t, False)
                for t in range(TPS):
                    attend(BATCH - 1, t, True)

                def hn_transpose(m):
                    pe.wait_ge(hn_ready, m + 1)
                    for t in range(TPS):
                        ins = pe.transpose(B[6][:, t * P:(t + 1) * P], hn[:, t, :], ident[:])
                    ins.then_inc(hnT_ready, 1)

                def up(m):
                    pe.wait_ge(hnT_copied, m + 1)
                    for j in range(NHC):
                        H = HSIZE[j]
                        pe.matmul(B[j][0:H, SEQ:2 * SEQ], w1_sb[:, HID + j * HC:HID + j * HC + H], hnT[:], start=True,
                                  stop=True)
                        pe.matmul(B[j][0:H, 0:SEQ], w1_sb[:, j * HC:j * HC + H], hnT[:], start=True,
                                  stop=True).then_inc(up_ready, 1)

                def down(m):
                    pe.wait_ge(seq_done, BATCH + m)
                    for j in range(NHC):
                        H = HSIZE[j]
                        pe.wait_ge(hid_ready, m * NHC + j + 1)
                        for t in range(TPS):
                            ins = pe.matmul(B[3 + t][:, 0:D], hidT[0:H, j, t * P:(t + 1) * P],
                                            w2_sb[0:H, bass.ds(l, 1), j, :].rearrange("p a d -> p (a d)"),
                                            start=j == 0, stop=j == NHC - 1)
                    ins.then_inc(down_ready, 1)

                pe.wait_ge(w1_loaded, 16 * l + 16)
                pe.wait_ge(x_done, n0 + NT)
                hn_transpose(l * BATCH)
                with pe.Fori(0, BATCH - 1) as s:
                    up(l * BATCH + s)
                    hn_transpose(l * BATCH + s + 1)
                    down(l * BATCH + s)
                up(l * BATCH + BATCH - 1)
                down(l * BATCH + BATCH - 1)


def constants():
    a, b = np.arange(WIN)[:, None], np.arange(WIN)[None, :]
    causal, band, none = b <= a, b >= a, np.zeros((WIN, WIN), bool)
    first = np.block([[causal, none], [band, causal]])
    second = np.block([[causal, band], [band, causal]])
    i, j = np.arange(SEQ)[:, None], np.arange(SEQ)[None, :]
    dec = j < i
    dec[0, 0] = True
    seen = np.concatenate([first] * 4 + [second] * 4 + [dec[:P, :P], dec[P:, :]], axis=1)
    masks = np.where(seen, 0.0, MASKED).astype(np.float32)

    half_idx = np.arange(0, DH, 2, dtype=np.float32)
    inv_freq = (np.float32(1.0) / np.float32(10000.0) ** (half_idx / np.float32(DH))).astype(np.float32)
    tok = np.arange(SEQ, dtype=np.float32)
    freqs = tok[:, None] * inv_freq[None, :]
    freqs = np.concatenate([freqs, freqs], axis=-1)
    base = (half_idx + np.float32(0.4 * DH)) / np.float32(1.4 * DH)
    power = (tok - SEQ // 2) / np.float32(WIN // 2)
    scale = base[None, :] ** power[:, None]
    scale = np.concatenate([scale, scale], axis=-1)
    sign = np.where(np.arange(DH) < DH // 2, -1.0, 1.0).astype(np.float32)
    cos, sin = np.cos(freqs), np.sin(freqs) * sign
    tables = np.stack([QK_SCALE * cos * scale, QK_SCALE * sin * scale, cos / scale, sin / scale])
    rope = tables.reshape(4, TPS, P, DH).transpose(2, 0, 1, 3)
    return (np.ascontiguousarray(rope, dtype=np.float32), np.ascontiguousarray(masks),
            np.eye(P, dtype=np.float32))


def kernel(**inputs):
    import concourse.bacc as bacc
    from concourse.bass_utils import run_bass_kernel_spmd

    g = {k: np.asarray(v) for k, v in inputs.items()}
    w2 = np.zeros((LAYERS, NHC * HC, D), np.float32)
    w2[:, :HID] = g["L0_ffn_w2"]
    b1 = np.zeros((LAYERS, 2, NHC * HC), np.float32)
    b1[:, :, :HID] = g["L0_ffn_b1"].reshape(LAYERS, 2, HID)
    q_s, k_s = g["L0_ffn_q_scale"], g["L0_ffn_k_scale"]
    rope, masks, identity = constants()
    arrays = {
        "x": g["L0_attn_hidden_states"].reshape(BATCH * SEQ, D),
        "w_dec": g["L0_attn_w_dec_attn"],
        "w_outT": g["L0_attn_w_out"].T.reshape(2, D, D).transpose(1, 0, 2),
        "b_out": g["L0_attn_b_out"],
        "wqkv": g["L0_ffn_wqkv"],
        "qk_scale": np.stack([q_s, np.roll(q_s, DH // 2, -1), k_s, np.roll(k_s, DH // 2, -1)], axis=1),
        "wo": g["L0_ffn_wo"].reshape(LAYERS, NCH, P, D).transpose(0, 2, 1, 3),
        "ln_gb": np.stack([g["L0_ffn_ln_g"], g["L0_ffn_ln_b"]], axis=-1).transpose(1, 0, 2),
        "w1": g["L0_ffn_w1"],
        "b1": b1.reshape(LAYERS, 2 * NHC, HC).transpose(2, 0, 1),
        "w2": w2.reshape(LAYERS, NHC, HC, D).transpose(2, 0, 1, 3),
        "b2": g["L0_ffn_b2"],
        "rope": rope,
        "masks": masks,
        "identity": identity,
    }
    arrays = {f"in_{k}": np.ascontiguousarray(v) for k, v in arrays.items()}
    nc = bacc.Bacc("TRN2", target_bir_lowering=False, num_devices=1)
    aps = [nc.dram_tensor(k, v.shape, mybir.dt.from_np(v.dtype), kind="ExternalInput").ap() for k, v in arrays.items()]
    out = nc.dram_tensor("out", (BATCH * SEQ, D), F32, kind="ExternalOutput").ap()
    program(nc, *aps, out)
    r = run_bass_kernel_spmd(nc, [arrays], core_ids=[0])
    return r.results[0]["out"].reshape(BATCH, SEQ, D)
```

```python
import numpy as np
import concourse.bass as bass
from concourse import mybir
from contextlib import ExitStack

F32 = mybir.dt.float32
BF16 = mybir.dt.bfloat16
F32R = mybir.dt.float32r
ALU = mybir.AluOpType
ACT = mybir.ActivationFunctionType
AXX = mybir.AxisListType.X

P = 128
BATCH = 16
SEQ = 256
TPS = SEQ // P
NT = BATCH * TPS
D = 128
HALF = D // 2
LAYERS = 2
HEADS = 8
DH = 64
INNER = HEADS * DH
WIN = 64
NCH = INNER // P
HID = int(D * 4 * 2 / 3)
HC = 114
NHC = 3
HSIZE = [HC, HC, HID - 2 * HC]
EPS = 1e-5
MASKED = -(2.0 ** 126)
QK_SCALE = 8.0


def program(nc, x, w_dec, w_outT, b_out, wqkv, qk_scale, wo, ln_gb, w1, b1, w2, b2,
            rope, masks, identity, out):
    with ExitStack() as ctx:
        def sb(name, shape, dt=F32):
            return ctx.enter_context(nc.sbuf_tensor(name, shape, dt))

        def sem(name):
            return ctx.enter_context(nc.semaphore(name))

        x_in = sb("x_in", [P, NT, D])
        x_res = sb("x_res", [P, NT, D])
        s_all = sb("s_all", [P, NT, D])
        h_shift = sb("h_shift", [P, NT, HALF])
        ident = sb("ident", [P, P])
        ident_bf = sb("ident_bf", [P, P], BF16)
        mask_f32 = sb("mask_f32", [P, 2 * 4 * P + 3 * P])
        mask_sb = sb("mask_sb", [P, 2 * 4 * P + 3 * P], BF16)
        win_mask = [mask_sb[:, t * 4 * P:(t + 1) * 4 * P] for t in range(TPS)]
        dec_mask = mask_sb[:, 8 * P:11 * P]
        rope_sb = sb("rope_sb", [P, 4, TPS, DH])
        rope_l = sb("rope_l", [P, 4, TPS, DH])
        qk_scale_sb = sb("qk_scale_sb", [P, LAYERS, 4, DH])
        w_dec_sb = sb("w_dec_sb", [P, D])
        w_out_sb = sb("w_out_sb", [P, 2, D])
        b_out_sb = sb("b_out_sb", [P, D])
        wqkv_hi = sb("wqkv_hi", [P, LAYERS, 3 * INNER], F32R)
        wqkv_lo = sb("wqkv_lo", [P, LAYERS, 3 * INNER], F32R)
        wo_sb = sb("wo_sb", [P, LAYERS, NCH, D])
        ln_sb = sb("ln_sb", [P, LAYERS, 2])
        w1_sb = sb("w1_sb", [P, 2 * HID])
        w1_hi = sb("w1_hi", [P, 2 * HID], F32R)
        w1_lo = sb("w1_lo", [P, 2 * HID], F32R)
        b1_sb = sb("b1_sb", [HC, LAYERS, 2 * NHC])
        ln_l = sb("ln_l", [P, 2])
        b1_l = sb("b1_l", [HC, 2 * NHC])
        w2_sb = sb("w2_sb", [HC, LAYERS, NHC, D])
        b2_sb = sb("b2_sb", [P, LAYERS, D])
        minus_half = sb("minus_half", [P, 2 * HEADS])
        zero = sb("zero", [P, 1])
        stats = sb("stats", [P, TPS, 12])
        mean_var = sb("mean_var", [P, TPS, 2])
        var_eps = sb("var_eps", [P, TPS])
        rstd = sb("rstd", [P, TPS])
        xn = sb("xn", [P, TPS, D])
        xnT = sb("xnT", [P, 2, SEQ])
        dq = sb("dq", [P, SEQ])
        d_nmax = sb("d_nmax", [P, TPS])
        d_den = sb("d_den", [P, TPS])
        d_rden = sb("d_rden", [P, TPS])
        dp = sb("dp", [P, 3 * P])
        dpT = sb("dpT", [P, 3 * P])
        dctx = sb("dctx", [P, TPS, D])
        dctxT = sb("dctxT", [P, SEQ])
        x_stage = sb("x_stage", [P, TPS, D])
        hT = sb("hT", [P, SEQ + 1])
        hT_hi = sb("hT_hi", [P, TPS, P], F32R)
        hT_lo = sb("hT_lo", [P, TPS, P], F32R)
        sq = sb("sq", [P, 2 * HEADS, DH])
        ssq = sb("ssq", [P, 2 * HEADS])
        ssq_c = sb("ssq_c", [P, 2 * HEADS])
        rnorm = sb("rnorm", [P, TPS, 2 * HEADS])
        qa = sb("qa", [P, INNER])
        qb = sb("qb", [P, INNER])
        qrot = sb("qrot", [P, INNER])
        kab = sb("kab", [P, INNER])
        ka = sb("ka", [P, INNER])
        kb = sb("kb", [P, INNER])
        krot = sb("krot", [P, INNER])
        qT = sb("qT", [P, NCH, P])
        kT = sb("kT", [P, NCH, SEQ])
        v_sb = sb("v_sb", [P, TPS, INNER])
        v_mid = sb("v_mid", [P, INNER])
        smax = sb("smax", [P, 2, 4])
        nbias = sb("nbias", [P, 2, 4])
        prob = sb("prob", [P, 2, 4 * P])
        den = sb("den", [P, 2, 4])
        rden = sb("rden", [P, 2, 4])
        pT = sb("pT", [P, 2, 4 * P])
        oT = sb("oT", [P, NCH, P])
        hn = sb("hn", [P, TPS, D])
        hnT = sb("hnT", [P, SEQ])
        hnT_hi = sb("hnT_hi", [P, 2, SEQ], F32R)
        hnT_lo = sb("hnT_lo", [P, 2, SEQ], F32R)
        gl = sb("gl", [HC, NHC, SEQ])
        hidT = sb("hidT", [HC, 2, NHC, SEQ])
        gate = sb("gate", [P, NT // 4, 4 * D])
        wqkv_sb = gate[:, 0:LAYERS * 3, :].rearrange("p (l i) f -> p l (i f)", l=LAYERS)

        psum = ctx.enter_context(nc.psum_tensor("psum", [P, 8, 512], F32))
        B = [psum[:, i, :] for i in range(8)]

        seq_done = sem("seq_done")
        x_loaded = [sem(f"x_loaded{i}") for i in range(3)]
        dec_loaded = sem("dec_loaded")
        const_loaded = sem("const_loaded")
        w1_loaded = sem("w1_loaded")
        w1_rounded = sem("w1_rounded")
        w1_split = sem("w1_split")
        half_made = sem("half_made")
        masks_made = sem("masks_made")
        shifted = sem("shifted")
        aggregated = sem("aggregated")
        var_made = sem("var_made")
        rstd_made = sem("rstd_made")
        xn_ready = sem("xn_ready")
        xn_saved = sem("xn_saved")
        xnT_ready = sem("xnT_ready")
        xnT_copied = sem("xnT_copied")
        dq_ready = sem("dq_ready")
        dq_copied = sem("dq_copied")
        ds_ready = sem("ds_ready")
        dmax_ready = sem("dmax_ready")
        dp_ready = sem("dp_ready")
        drden_ready = sem("drden_ready")
        dpT_ready = sem("dpT_ready")
        dpT_copied = sem("dpT_copied")
        dctx_ready = sem("dctx_ready")
        dctx_scaled = sem("dctx_scaled")
        dctxT_ready = sem("dctxT_ready")
        dctxT_copied = sem("dctxT_copied")
        dout_ready = sem("dout_ready")
        tanh_done = sem("tanh_done")
        w_rounded = sem("w_rounded")
        w_split = sem("w_split")
        tables_ready = sem("tables_ready")
        x_staged = sem("x_staged")
        xT_ready = sem("xT_ready")
        hT_ready = sem("hT_ready")
        hT_hi_ready = sem("hT_hi_ready")
        hT_split = sem("hT_split")
        q_ready = sem("q_ready")
        k_ready = sem("k_ready")
        v_ready = sem("v_ready")
        sq_ready = sem("sq_ready")
        ssq_summed = sem("ssq_summed")
        ssq_ready = sem("ssq_ready")
        rnorm_ready = sem("rnorm_ready")
        qab_ready = sem("qab_ready")
        k_summed = sem("k_summed")
        kab_ready = sem("kab_ready")
        qrot_ready = sem("qrot_ready")
        krot_ready = sem("krot_ready")
        qT_ready = sem("qT_ready")
        qT_copied = sem("qT_copied")
        kT_ready = sem("kT_ready")
        kT_copied = sem("kT_copied")
        v_copied = sem("v_copied")
        vmid_ready = sem("vmid_ready")
        s_ready = sem("s_ready")
        smax_ready = sem("smax_ready")
        nbias_ready = sem("nbias_ready")
        p_ready = sem("p_ready")
        pTe_ready = sem("pTe_ready")
        pTe_copied = sem("pTe_copied")
        pTo_ready = sem("pTo_ready")
        pTo_copied = sem("pTo_copied")
        o_ready = sem("o_ready")
        rden_ready = sem("rden_ready")
        pn_ready = sem("pn_ready")
        oT_copied = sem("oT_copied")
        y_ready = sem("y_ready")
        x_done = sem("x_done")
        hn_ready = sem("hn_ready")
        hnT_ready = sem("hnT_ready")
        hnT_copied = sem("hnT_copied")
        hnT_split = sem("hnT_split")
        up_ready = sem("up_ready")
        gelu_ready = sem("gelu_ready")
        hid_ready = sem("hid_ready")
        b2_added = sem("b2_added")
        down_ready = sem("down_ready")
        silu_ready = sem("silu_ready")
        pool_gated = sem("pool_gated")
        dve_gated = sem("dve_gated")
        pool_done = sem("pool_done")
        dve_done = sem("dve_done")
        stored = sem("stored")

        N_DEC = 5
        N_CONST = 11
        CHUNKS = [(0, 1), (1, 4), (4, BATCH)]
        POOL_CHUNKS = [0, 1, 2]
        DVE_CHUNKS = [3, 4, 5, 6, 7]
        STORED = [0, 3, 4, 1, 5, 6, 2, 7]

        def tile(buf, n):
            return buf[:, bass.ds(n, 1), :].rearrange("p a d -> p (a d)")

        def pair(buf, s):
            return buf[:, bass.ds(TPS * s, TPS), :]

        def heads(ap):
            return ap.rearrange("p (h e) -> p h e", e=DH)

        def peeled_at(s, turns):
            return isinstance(s, int) and s in turns

        def swapped(ap):
            return ap.rearrange("p (h k e) -> p h k e", k=2, e=DH // 2)[:, :, ::-1, :]

        def table(i, t):
            return rope_l[:, i, t, :].unsqueeze(1).broadcast_to([P, HEADS, DH])

        def table2(i, t):
            return rope_l[:, i, t, :].rearrange("p (k e) -> p k e", k=2).unsqueeze(1).broadcast_to(
                [P, HEADS, 2, DH // 2])

        def dec_pipeline(engine, turn):
            def peeled(s):
                turn(s, s % 2, {k for k in range(-1, 5) if 0 <= s + k < BATCH})

            for s in range(-4, 2):
                peeled(s)
            with engine.Fori(1, BATCH // 2 - 2) as i:
                for parity in range(2):
                    turn(2 * i + parity, parity, {-1, 0, 1, 2, 3, 4})
            for s in range(BATCH - 4, BATCH + 1):
                peeled(s)

        def pipeline(engine, turn):
            turn(-2, 1, {3})
            turn(-1, 0, {2, 3, 4})
            turn(-1, 1, {1, 2, 3, 4})
            with engine.Fori(0, BATCH - TPS) as s:
                for t in range(TPS):
                    turn(s, t, {0, 1, 2, 3, 4})
            turn(BATCH - 2, 0, {0, 1, 2, 3})
            turn(BATCH - 2, 1, {0, 1, 2})
            turn(BATCH - 1, 0, {0, 1})
            turn(BATCH - 1, 1, {0})

        def q_sum(engine, n, first):
            engine.wait_ge(qab_ready, n + 1)
            if not first:
                engine.wait_ge(qT_ready, n)
            engine.tensor_tensor(qrot[:], qa[:], qb[:], ALU.add).then_inc(qrot_ready, 1)

        def k_sum(engine, t, n, first):
            engine.wait_ge(kab_ready, n + 1)
            if not first:
                engine.wait_ge(kT_ready, n)
            engine.tensor_tensor(kab[:], ka[:], kb[:], ALU.add).then_inc(k_summed, 1)
            engine.wait_ge(k_summed, n + 1)
            engine.wait_ge(rnorm_ready, n + 1)
            engine.tensor_tensor(heads(krot[:]), heads(kab[:]),
                                 rnorm[:, t, HEADS:2 * HEADS].unsqueeze(2).broadcast_to([P, HEADS, DH]),
                                 ALU.mult).then_inc(krot_ready, 1)

        def ffn_pipeline(engine, turn, begin=-4):
            def peeled(s):
                turn(s, s % 2, {k for k in range(5) if 0 <= s + k < BATCH})

            for s in range(begin, 0):
                peeled(s)
            with engine.Fori(0, BATCH // 2 - 2) as i:
                for parity in range(2):
                    turn(2 * i + parity, parity, {0, 1, 2, 3, 4})
            for s in range(BATCH - 4, BATCH):
                peeled(s)

        def four(buf, c):
            return buf[:, 4 * c:4 * c + 4, :].rearrange("p n d -> p (n d)")

        def final(engine, chunks, gated, done):
            engine.wait_ge(tanh_done, BATCH)
            for c, before in zip(chunks + [None], [None] + chunks):
                if c is not None:
                    engine.wait_ge(silu_ready, c + 1)
                    engine.tensor_tensor(gate[:, c, :], gate[:, c, :], four(s_all, c),
                                         ALU.mult).then_inc(gated, 1)
                if before is not None:
                    engine.wait_ge(gated, chunks.index(before) + 1)
                    engine.tensor_tensor(gate[:, before, :], gate[:, before, :], four(x_in, before),
                                         ALU.add).then_inc(done, 1)

        block = ctx.enter_context(nc.Block())

        @block.sync
        def _(sp):
            def load_x(i):
                a, b = CHUNKS[i]
                sp.dma_start(x_in[:, a * TPS:b * TPS, :],
                             x.rearrange("(n p) d -> p n d", p=P)[:, a * TPS:b * TPS, :]).then_inc(x_loaded[i], 16)

            load_x(0)
            dec_loads = [(ident[:], identity), (w_dec_sb[:], w_dec), (mask_f32[:, 8 * P:], masks[:, 8 * P:]),
                         (w_out_sb[:], w_outT), (b_out_sb[:], b_out.partition_broadcast(P))]
            assert len(dec_loads) == N_DEC
            for dst, src in dec_loads:
                sp.dma_start(dst, src).then_inc(dec_loaded, 16)
            load_x(1)
            load_x(2)
            loads = [
                (mask_f32[:, 0:8 * P], masks[:, 0:8 * P]), (rope_sb[:], rope),
                (qk_scale_sb[:], qk_scale.partition_broadcast(P)),
                (wqkv_sb[:, 0, :], wqkv[0]), (wqkv_sb[:, 1, :], wqkv[1]), (wo_sb[:, 0], wo[0]), (wo_sb[:, 1], wo[1]),
                (ln_sb[:], ln_gb), (b1_sb[:], b1), (w2_sb[:], w2), (b2_sb[:], b2.partition_broadcast(P)),
            ]
            assert len(loads) == N_CONST
            for dst, src in loads:
                sp.dma_start(dst, src).then_inc(const_loaded, 16)
            with sp.Fori(0, LAYERS) as l:
                sp.wait_ge(seq_done, l * BATCH + BATCH)
                sp.dma_start(w1_sb[:], w1[bass.ds(l, 1)].rearrange("a p f -> (a p) f")).then_inc(w1_loaded, 16)
                with sp.Fori(0, BATCH) as s:
                    m = l * BATCH + s
                    sp.wait_ge(shifted, m * 32 + 32)
                    sp.wait_ge(x_done, m * TPS + TPS)
                    sp.dma_start(h_shift[1:P, bass.ds(TPS * s, TPS), :],
                                 x_res[0:P - 1, bass.ds(TPS * s, TPS), HALF:D]).then_inc(shifted, 16)
                    sp.dma_start(h_shift[0:1, bass.ds(TPS * s + 1, 1), :],
                                 x_res[P - 1:P, bass.ds(TPS * s, 1), HALF:D]).then_inc(shifted, 16)
            for c in STORED:
                if c in DVE_CHUNKS:
                    sp.wait_ge(dve_done, DVE_CHUNKS.index(c) + 1)
                else:
                    sp.wait_ge(pool_done, POOL_CHUNKS.index(c) + 1)
                sp.dma_start(out.rearrange("(n p) d -> p n d", p=P)[:, 4 * c:4 * c + 4, :],
                             gate[:, c, :].rearrange("p (n d) -> p n d", n=4)).then_inc(stored, 16)
            sp.wait_ge(stored, 16 * (NT // 4))

        @block.gpsimd
        def _(pool):
            pool.wait_ge(half_made, 1)

            def inverse_std(i):
                pool.wait_ge(var_made, i + 1)
                pool.tensor_tensor(rstd[:], var_eps[:], minus_half[:, 0:TPS], ALU.pow).then_inc(rstd_made, 1)

            def dec_turn(s, parity, steps):
                if 3 in steps:
                    pool.wait_ge(xn_ready, s + 4)
                    pool.tensor_copy(pair(x_res, s + 3), xn[:]).then_inc(xn_saved, 1)
                if 4 in steps:
                    inverse_std(s + 4)

            dec_pipeline(pool, dec_turn)
            pool.wait_ge(const_loaded, 16 * N_CONST)

            def inverse_norms(t, n, first):
                pool.wait_ge(ssq_ready, n + 1)
                if not first:
                    pool.wait_ge(p_ready, 2 * n - 2)
                pool.tensor_tensor(rnorm[:, t, :], ssq_c[:], minus_half[:], ALU.pow).then_inc(rnorm_ready, 1)

            def split_h(t, n, first):
                pool.wait_ge(hT_ready, n + 1)
                if not first:
                    pool.wait_ge(v_ready, n - 1)
                h = hT[:, t * P:(t + 1) * P]
                pool.tensor_tensor(hT_hi[:, t, :], h, zero[:].broadcast_to([P, P]), ALU.add).then_inc(hT_hi_ready, 1)
                pool.wait_ge(hT_hi_ready, n + 1)
                pool.tensor_tensor(hT_lo[:, t, :], h, hT_hi[:, t, :], ALU.subtract).then_inc(hT_split, 1)

            with pool.Fori(0, LAYERS) as l:
                n0 = l * NT
                pool.wait_ge(seq_done, l * BATCH + BATCH - 4)
                pool.tensor_copy(x_stage[:], x_res[:, 0:TPS, :]).then_inc(x_staged, TPS)

                def turn(s, t, steps):
                    n = n0 + TPS * s + t
                    if 1 not in steps and 3 in steps:
                        split_h(1 - t, n + 3, first=True)
                    if 2 in steps:
                        inverse_norms(t, n + 2, first=0 not in steps)
                    if 1 in steps and 3 in steps:
                        split_h(1 - t, n + 3, first=False)
                    if 2 in steps and 1 in steps:
                        q_sum(pool, n + 2, first=False)
                        k_sum(pool, t, n + 2, first=False)

                pipeline(pool, turn)

                def ffn_turn(s, parity, steps):
                    m = l * BATCH + s
                    if 2 in steps:
                        pool.wait_ge(hnT_copied, m + 3)
                        pool.tensor_tensor(hnT_lo[:, parity, :], hnT[:], hnT_hi[:, parity, :],
                                           ALU.subtract).then_inc(hnT_split, 1)
                        pool.tensor_tensor(pair(x_res, s + 2), pair(x_res, s + 2),
                                           b2_sb[:, bass.ds(l, 1), :].broadcast_to([P, TPS, D]),
                                           ALU.add).then_inc(b2_added, 1)
                    if 4 in steps:
                        inverse_std(m + 4 + BATCH)

                ffn_pipeline(pool, ffn_turn)
            final(pool, POOL_CHUNKS, pool_gated, pool_done)

        @block.scalar
        def _(act):
            act.wait_ge(dec_loaded, 16 * N_DEC)
            act.activation(mask_sb[:, 8 * P:], mask_f32[:, 8 * P:], ACT.Copy)
            act.activation(ident_bf[:], ident[:], ACT.Copy).then_inc(masks_made, 1)

            def round_weights(k):
                l, i = divmod(k, 3)
                w = slice(i * INNER, (i + 1) * INNER)
                act.activation(wqkv_hi[:, l, w], wqkv_sb[:, l, w], ACT.Copy).then_inc(w_rounded, 1)

            def dec_turn(s, parity, steps):
                if peeled_at(s, [BATCH - 1]):
                    act.activation(mask_sb[:, 0:8 * P], mask_f32[:, 0:8 * P], ACT.Copy).then_inc(masks_made, 1)
                if peeled_at(s, range(BATCH - 4, BATCH - 1)):
                    act.wait_ge(const_loaded, 16 * N_CONST)
                    for k in range(2):
                        round_weights(2 * (s - BATCH + 4) + k)
                if 2 in steps:
                    act.wait_ge(xnT_ready, s + 3)
                    act.activation(xnT[:, parity, :], B[0][:, 0:SEQ], ACT.Copy).then_inc(xnT_copied, 1)
                if 0 in steps:
                    act.wait_ge(dpT_ready, s + 1)
                    act.activation(dpT[:], B[3][:, 0:3 * P], ACT.Copy).then_inc(dpT_copied, 1)
                if -1 in steps:
                    act.wait_ge(seq_done, s)
                    act.activation(pair(s_all, s - 1), pair(s_all, s - 1), ACT.Tanh).then_inc(tanh_done, 1)
                if 1 in steps:
                    act.wait_ge(dmax_ready, s + 2)
                    for t in range(TPS):
                        a, b = t * P, t * P + (t + 1) * P
                        ins = act.activation(dp[:, a:b], B[2][:, a:b], ACT.Exp, bias=d_nmax[:, t:t + 1],
                                             accum_out=d_den[:, t:t + 1])
                    ins.then_inc(dp_ready, 1)
                if 2 in steps:
                    act.wait_ge(dq_ready, s + 3)
                    act.activation(dq[:], B[1][:, 0:SEQ], ACT.Copy).then_inc(dq_copied, 1)
                if 0 in steps:
                    act.wait_ge(dctxT_ready, s + 1)
                    act.activation(dctxT[:], B[5][:, 0:SEQ], ACT.Copy).then_inc(dctxT_copied, 1)

            dec_pipeline(act, dec_turn)

            def stage(s, t, n):
                act.wait_ge(xT_ready, n - TPS + 1)
                act.activation(x_stage[:, t, :], tile(x_res, TPS * s + t), ACT.Copy).then_inc(x_staged, 1)

            def token_shift(t, n, first):
                if not first:
                    act.wait_ge(hT_split, n)
                act.wait_ge(xT_ready, n + 1)
                act.activation(hT[0:HALF, t * P:(t + 1) * P], B[5][0:HALF, 0:P], ACT.Copy)
                act.activation(hT[HALF:P, t * P + 1:(t + 1) * P + 1], B[5][HALF:P, 0:P],
                               ACT.Copy).then_inc(hT_ready, 1)

            def squares(n, i, first):
                if not first:
                    act.wait_ge(ssq_summed, 2 * n - 1 + i)
                act.wait_ge((q_ready, k_ready)[i], n + 1)
                act.activation(sq[:, i * HEADS:(i + 1) * HEADS, :], heads(B[i]), ACT.Square).then_inc(sq_ready, 1)

            def values(t, n, first, vmid_count):
                act.wait_ge(v_ready, n + 1)
                if not first:
                    act.wait_ge(o_ready, n - 1)
                    if t == 0:
                        act.wait_ge(vmid_ready, vmid_count)
                act.activation(v_sb[:, t, :], B[2], ACT.Copy).then_inc(v_copied, 1)

            def q_transposed(n):
                act.wait_ge(qT_ready, n + 1)
                act.activation(qT[:].rearrange("p c n -> p (c n)"), B[6], ACT.Copy).then_inc(qT_copied, 1)

            def k_transposed(t, n):
                act.wait_ge(kT_ready, n + 1)
                act.activation(kT[:, :, t * P:(t + 1) * P], B[5].rearrange("p (c n) -> p c n", c=NCH),
                               ACT.Copy).then_inc(kT_copied, 1)

            def exps(t, n, e):
                act.wait_ge(nbias_ready, 2 * n + e + 1)
                for j in range(4):
                    h = 2 * j + e
                    ins = act.activation(prob[:, e, j * P:(j + 1) * P], B[3 + e][:, j * P:(j + 1) * P], ACT.Exp,
                                         bias=nbias[:, e, j:j + 1], scale=rnorm[:, t, h:h + 1],
                                         accum_out=den[:, e, j:j + 1])
                ins.then_inc(p_ready, 1)

            with act.Fori(0, LAYERS) as l:
                n0 = l * NT
                act.wait_ge(xn_saved, BATCH)
                act.wait_ge(seq_done, l * BATCH + BATCH - 4)

                def turn(s, t, steps):
                    n = n0 + TPS * s + t
                    u = 1 - t
                    if 0 in steps:
                        act.wait_ge(pTe_ready, n + 1)
                        act.activation(pT[:, 0, :], B[6], ACT.Copy).then_inc(pTe_copied, 1)
                        act.wait_ge(pTo_ready, n + 1)
                        act.activation(pT[:, 1, :], B[2], ACT.Copy).then_inc(pTo_copied, 1)
                    if 1 in steps and 0 not in steps:
                        act.wait_ge(seq_done, l * BATCH + BATCH)
                    if 1 in steps and 2 not in steps:
                        act.wait_ge(w1_loaded, 16 * l + 16)
                        act.activation(w1_hi[:], w1_sb[:], ACT.Copy).then_inc(w1_rounded, 1)
                    if 3 in steps:
                        token_shift(u, n + 3, first=1 not in steps)
                    if 4 in steps:
                        stage(s + 2, t, n + 4)
                    if 1 in steps:
                        exps(u, n + 1, 0)
                        exps(u, n + 1, 1)
                    if 3 in steps:
                        squares(n + 3, 0, first=2 not in steps)
                        squares(n + 3, 1, first=2 not in steps)
                    if 2 in steps:
                        q_transposed(n + 2)
                        values(t, n + 2, first=0 not in steps, vmid_count=l * BATCH + s + 1)
                        k_transposed(t, n + 2)

                pipeline(act, turn)

                def gelu(m, j):
                    act.wait_ge(up_ready, m * NHC + j + 1)
                    H = HSIZE[j]
                    act.activation(gl[0:H, j, :], B[j][0:H, SEQ:2 * SEQ], ACT.Gelu,
                                   bias=b1_l[0:H, NHC + j:NHC + j + 1]).then_inc(gelu_ready, 1)

                def ffn_turn(s, parity, steps):
                    m = l * BATCH + s
                    if 0 in steps:
                        gelu(m, 2)
                    if 2 in steps:
                        if 1 in steps:
                            act.wait_ge(hnT_split, m + 2)
                        act.wait_ge(hnT_ready, m + 3)
                        for dst in (hnT[:], hnT_hi[:, parity, :]):
                            ins = act.activation(dst, B[6][:, 0:SEQ], ACT.Identity, bias=ln_l[:, 1:2],
                                                 scale=ln_l[:, 0:1])
                        ins.then_inc(hnT_copied, 1)
                    if 1 in steps:
                        gelu(m + 1, 0)
                        gelu(m + 1, 1)

                ffn_pipeline(act, ffn_turn)

            for c in range(NT // 4):
                act.wait_ge(seq_done, LAYERS * BATCH + (c + 1) * 4 // TPS)
                act.activation(gate[:, c, :], x_res[:, 4 * c:4 * c + 4, :].rearrange("p n d -> p (n d)"),
                               ACT.Silu).then_inc(silu_ready, 1)

        @block.vector
        def _(dve):
            dve.memset(hT[HALF:P, 0:1], 0.0)
            dve.memset(zero[:], 0.0)
            dve.memset(minus_half[:], -0.5).then_inc(half_made, 1)
            dve.memset(h_shift[0:1, :, :], 0.0).then_inc(shifted, 32)

            def norm_scale(dst, src, t, inc=None):
                ins = dve.tensor_scalar(dst, src, mean_var[:, t, 0:1], rstd[:, t:t + 1], ALU.subtract, ALU.mult)
                if inc is not None:
                    ins.then_inc(inc, 1)

            def dec_stats(s):
                for i, (begin, _) in enumerate(CHUNKS):
                    if peeled_at(s, [begin]):
                        dve.wait_ge(x_loaded[i], 16)
                for t in range(TPS):
                    ins = dve.bn_stats(stats[:, t, 0:6], tile(x_in, TPS * s + t))
                dve.drain()
                for t in range(TPS):
                    ins = dve.bn_aggr(mean_var[:, t, :], stats[:, t, 0:6])
                ins.then_inc(aggregated, 1)
                dve.wait_ge(aggregated, s + 1)
                dve.tensor_scalar(var_eps[:], mean_var[:, :, 1], EPS, None, ALU.add).then_inc(var_made, 1)

            def dec_norm(s, first):
                dve.wait_ge(rstd_made, s + 1)
                if not first:
                    dve.wait_ge(xnT_ready, s)
                    dve.wait_ge(xn_saved, s)
                norm_scale(xn[:, 0, :], tile(x_in, TPS * s), 0)
                norm_scale(xn[:, 1, :], tile(x_in, TPS * s + 1), 1, xn_ready)

            def dec_max(s):
                dve.wait_ge(ds_ready, s + 1)
                for t in range(TPS):
                    a, b = t * P, t * P + (t + 1) * P
                    ins = dve.tensor_reduce(d_nmax[:, t:t + 1], B[2][:, a:b], AXX, ALU.max, negate=True)
                ins.then_inc(dmax_ready, 1)

            def dec_turn(s, parity, steps):
                if 0 in steps:
                    if -1 in steps:
                        dve.wait_ge(dctx_scaled, s)
                    dve.wait_ge(dp_ready, s + 1)
                    dve.reciprocal(d_rden[:], d_den[:]).then_inc(drden_ready, 1)
                if -1 in steps:
                    if peeled_at(s, [1]):
                        dve.wait_ge(dec_loaded, 16 * N_DEC)
                    dve.wait_ge(dout_ready, s)
                    dve.tensor_tensor(pair(s_all, s - 1),
                                      B[7 - parity][:, 0:SEQ].rearrange("p (t d) -> p t d", t=TPS),
                                      b_out_sb[:].unsqueeze(1).broadcast_to([P, TPS, D]),
                                      ALU.add).then_inc(seq_done, 1)
                if 3 in steps:
                    dec_norm(s + 3, first=2 not in steps)
                if 1 in steps:
                    dec_max(s + 1)
                if 0 in steps:
                    dve.wait_ge(drden_ready, s + 1)
                    dve.wait_ge(dctx_ready, s + 1)
                    for t in range(TPS):
                        ins = dve.tensor_scalar(dctx[:, t, :], B[4][:, t * D:(t + 1) * D], d_rden[:, t:t + 1], None,
                                                ALU.mult)
                    ins.then_inc(dctx_scaled, 1)
                if 4 in steps:
                    dec_stats(s + 4)
                if peeled_at(s, range(BATCH - 3, BATCH)):
                    for k in range(2):
                        rest_of_weights(2 * (s - BATCH + 3) + k)

            def rest_of_weights(k):
                l, i = divmod(k, 3)
                w = slice(i * INNER, (i + 1) * INNER)
                dve.wait_ge(w_rounded, k + 1)
                dve.tensor_tensor(wqkv_lo[:, l, w], wqkv_sb[:, l, w], wqkv_hi[:, l, w],
                                  ALU.subtract).then_inc(w_split, 1)

            dec_pipeline(dve, dec_turn)
            dve.wait_ge(const_loaded, 16 * N_CONST)

            def sums(n, first):
                for i in range(2):
                    dve.wait_ge(sq_ready, 2 * n + i + 1)
                    of = slice(i * HEADS, (i + 1) * HEADS)
                    dve.tensor_reduce(ssq[:, of], sq[:, of, :], AXX, ALU.add).then_inc(ssq_summed, 1)
                dve.wait_ge(ssq_summed, 2 * n + 2)
                if not first:
                    dve.wait_ge(rnorm_ready, n)
                dve.tensor_scalar(ssq_c[:], ssq[:], 1e-24, None, ALU.max).then_inc(ssq_ready, 1)

            def rope_q(t, n, first):
                dve.wait_ge(sq_ready, 2 * n + 1)
                if not first:
                    dve.wait_ge(qrot_ready, n)
                dve.tensor_tensor(heads(qa[:]), heads(B[0]), table(0, t), ALU.mult)
                dve.tensor_tensor(qb[:].rearrange("p (h k e) -> p h k e", k=2, e=DH // 2), swapped(B[0]),
                                  table2(1, t), ALU.mult).then_inc(qab_ready, 1)

            def rope_k_cos(t, n, first):
                dve.wait_ge(sq_ready, 2 * n + 2)
                if not first:
                    dve.wait_ge(k_summed, n)
                dve.tensor_tensor(heads(ka[:]), heads(B[1]), table(2, t), ALU.mult)

            def rope_k_sin(t, n):
                dve.tensor_tensor(kb[:].rearrange("p (h k e) -> p h k e", k=2, e=DH // 2), swapped(B[1]),
                                  table2(3, t), ALU.mult).then_inc(kab_ready, 1)

            def middle_values(n):
                dve.wait_ge(v_copied, n + 1)
                dve.tensor_copy(v_mid[0:WIN, :], v_sb[0:WIN, 1, :])
                dve.tensor_copy(v_mid[WIN:P, :], v_sb[WIN:P, 0, :]).then_inc(vmid_ready, 1)

            def maxima(t, n, e):
                dve.wait_ge(s_ready, 2 * n + e + 1)
                dve.tensor_reduce(smax[:, e, :], B[3 + e].rearrange("p (j k) -> p j k", j=4), AXX,
                                  ALU.max).then_inc(smax_ready, 1)
                dve.wait_ge(smax_ready, 2 * n + e + 1)
                dve.scalar_tensor_tensor(out=nbias[:, e, :], in0=smax[:, e, :], scalar=-1.0,
                                         in1=rnorm[:, t, e:HEADS:2], op0=ALU.mult,
                                         op1=ALU.mult).then_inc(nbias_ready, 1)

            def normed_probs(n, e):
                dve.wait_ge(p_ready, 2 * n + e + 1)
                dve.reciprocal(rden[:, e, :], den[:, e, :]).then_inc(rden_ready, 1)
                dve.wait_ge(rden_ready, 2 * n + e + 1)
                pr = prob[:, e, :].rearrange("p (j k) -> p j k", j=4)
                dve.tensor_tensor(pr, pr, rden[:, e, :].unsqueeze(2).broadcast_to([P, 4, P]),
                                  ALU.mult).then_inc(pn_ready, 1)

            with dve.Fori(0, LAYERS) as l:
                n0 = l * NT
                dve.wait_ge(seq_done, l * BATCH + BATCH)
                for i in range(4):
                    dve.tensor_tensor(rope_l[:, i], rope_sb[:, i],
                                      qk_scale_sb[:, bass.ds(l, 1), i, :].broadcast_to([P, TPS, DH]), ALU.mult)
                dve.tensor_copy(ln_l[:], tile(ln_sb, l))
                dve.tensor_copy(b1_l[:], tile(b1_sb, l)).then_inc(tables_ready, 1)
                dve.wait_ge(tables_ready, l + 1)

                def norm(s, m):
                    dve.wait_ge(shifted, 32 * m + 64)
                    dve.wait_ge(x_done, TPS * m + TPS)
                    for t in range(TPS):
                        dve.bn_stats(stats[:, t, 0:6],
                                     x_res[:, bass.ds(TPS * s + t, 1), 0:HALF].rearrange("p a d -> p (a d)"))
                        ins = dve.bn_stats(stats[:, t, 6:12], tile(h_shift, TPS * s + t))
                    dve.drain()
                    for t in range(TPS):
                        ins = dve.bn_aggr(mean_var[:, t, :], stats[:, t, :])
                    ins.then_inc(aggregated, 1)
                    dve.wait_ge(aggregated, BATCH + m + 1)
                    dve.tensor_scalar(var_eps[:], mean_var[:, :, 1], EPS, None, ALU.add).then_inc(var_made, 1)

                def norm_apply(s, m, first=False):
                    dve.wait_ge(rstd_made, BATCH + m + 1)
                    if not first:
                        dve.wait_ge(hnT_ready, m)
                    for t in range(TPS):
                        norm_scale(hn[:, t, 0:HALF],
                                   x_res[:, bass.ds(TPS * s + t, 1), 0:HALF].rearrange("p a d -> p (a d)"), t)
                        norm_scale(hn[:, t, HALF:D], tile(h_shift, TPS * s + t), t, hn_ready if t == TPS - 1 else None)

                def hidden(m, parity, j):
                    H = HSIZE[j]
                    dve.wait_ge(gelu_ready, m * NHC + j + 1)
                    dve.scalar_tensor_tensor(out=hidT[0:H, parity, j, :], in0=B[j][0:H, 0:SEQ],
                                             scalar=b1_l[0:H, j:j + 1],
                                             in1=gl[0:H, j, :], op0=ALU.add, op1=ALU.mult).then_inc(hid_ready, 1)

                def added(s, m):
                    dve.wait_ge(b2_added, m + 1)
                    dve.wait_ge(down_ready, m + 1)
                    xp = pair(x_res, s)
                    dve.tensor_tensor(xp, psum[:, 3:5, 0:D], xp, ALU.add).then_inc(seq_done, 1)

                def turn(s, t, steps):
                    n = n0 + TPS * s + t
                    u = 1 - t
                    if 1 in steps and t == 0:
                        middle_values(n + 1)
                    if 1 in steps and 2 not in steps:
                        norm(0, l * BATCH)
                    if 1 in steps:
                        maxima(u, n + 1, 0)
                    if 1 in steps and 2 not in steps:
                        norm_apply(0, l * BATCH, first=True)
                    if 2 in steps and 1 not in steps:
                        q_sum(dve, n + 2, first=True)
                    if 2 in steps:
                        rope_k_cos(t, n + 2, first=1 not in steps)
                    if 1 in steps:
                        maxima(u, n + 1, 1)
                    if 2 in steps:
                        rope_k_sin(t, n + 2)
                    if 2 in steps and 1 not in steps:
                        k_sum(dve, t, n + 2, first=True)
                    if 0 in steps and 1 not in steps:
                        norm(1, l * BATCH + 1)
                        dve.wait_ge(w1_rounded, l + 1)
                        dve.tensor_tensor(w1_lo[:], w1_sb[:], w1_hi[:], ALU.subtract).then_inc(w1_split, 1)
                    if 0 in steps:
                        dve.wait_ge(o_ready, n + 1)
                        dve.tensor_copy(oT[:].rearrange("p c n -> p (c n)"), B[7]).then_inc(oT_copied, 1)
                    if 1 in steps:
                        normed_probs(n + 1, 0)
                        normed_probs(n + 1, 1)
                    if 3 in steps:
                        sums(n + 3, first=2 not in steps)
                        rope_q(u, n + 3, first=2 not in steps)
                    if 0 in steps and 1 not in steps:
                        norm_apply(1, l * BATCH + 1)
                    if 0 in steps:
                        dve.wait_ge(y_ready, n + 1)
                        xt = tile(x_res, TPS * s + t)
                        dve.tensor_tensor(xt, B[7][:, 0:D], xt, ALU.add).then_inc(x_done, 1)
                    if 0 in steps and 1 not in steps:
                        norm(2, l * BATCH + 2)

                pipeline(dve, turn)

                def ffn_turn(s, parity, steps):
                    m = l * BATCH + s
                    if 0 in steps:
                        hidden(m, parity, 2)
                    if 3 in steps:
                        norm_apply(s + 3, m + 3)
                    if 1 in steps:
                        hidden(m + 1, 1 - parity, 0)
                    if 4 in steps:
                        norm(s + 4, m + 4)
                    if 0 in steps:
                        added(s, m)
                    if 1 in steps:
                        hidden(m + 1, 1 - parity, 1)

                ffn_pipeline(dve, ffn_turn, begin=-1)

            final(dve, DVE_CHUNKS, dve_gated, dve_done)

        @block.tensor
        def _(pe):
            pe.wait_ge(dec_loaded, 16 * N_DEC)

            def dec_turn(s, parity, steps):
                if 2 in steps:
                    pe.wait_ge(xn_ready, s + 3)
                    for t in range(TPS):
                        ins = pe.transpose(B[0][:, t * P:(t + 1) * P], xn[:, t, :], ident[:])
                    ins.then_inc(xnT_ready, 1)
                if 0 in steps:
                    pe.wait_ge(dp_ready, s + 1)
                    for c in range(3):
                        ins = pe.transpose(B[3][:, c * P:(c + 1) * P], dp[:, c * P:(c + 1) * P], ident[:])
                    ins.then_inc(dpT_ready, 1)
                if -1 in steps:
                    pe.wait_ge(dctxT_copied, s)
                    for t in range(TPS):
                        ins = pe.matmul(B[7 - parity][:, t * D:(t + 1) * D], dctxT[:, t * P:(t + 1) * P],
                                        w_out_sb[:, 1, :], start=False, stop=True, skip_group_check=True)
                    ins.then_inc(dout_ready, 1)
                if 1 in steps:
                    if 0 not in steps:
                        pe.wait_ge(masks_made, 1)
                    pe.wait_ge(dq_copied, s + 2)
                    pe.matmul(B[2][:, 0:3 * P], ident_bf[:], dec_mask, start=True, stop=False, skip_group_check=True)
                    for t in range(TPS):
                        a, b = t * P, t * P + (t + 1) * P
                        ins = pe.matmul(B[2][:, a:b], dq[:, t * P:(t + 1) * P], xnT[:, 1 - parity, 0:(t + 1) * P],
                                        start=False, stop=t == TPS - 1, skip_group_check=True)
                    ins.then_inc(ds_ready, 1)
                if 0 in steps:
                    pe.wait_ge(dpT_copied, s + 1)
                    pe.wait_ge(xn_saved, s + 1)
                    pe.matmul(B[4][:, 0:D], dpT[:, 0:P], tile(x_res, TPS * s), start=True, stop=True)
                    pe.matmul(B[4][:, D:2 * D], dpT[:, P:2 * P], tile(x_res, TPS * s), start=True, stop=False)
                    pe.matmul(B[4][:, D:2 * D], dpT[:, 2 * P:3 * P], tile(x_res, TPS * s + 1), start=False,
                              stop=True).then_inc(dctx_ready, 1)
                if 2 in steps:
                    pe.wait_ge(xnT_copied, s + 3)
                    pe.matmul(B[1][:, 0:SEQ], w_dec_sb[:], xnT[:, parity, :], start=True,
                              stop=True).then_inc(dq_ready, 1)
                if 1 in steps:
                    if -1 in steps:
                        pe.wait_ge(seq_done, s)
                    for t in range(TPS):
                        pe.matmul(B[7 - parity][:, t * D:(t + 1) * D], xnT[:, 1 - parity, t * P:(t + 1) * P],
                                  w_out_sb[:, 0, :], start=t == 0, stop=False, skip_group_check=True)
                if 0 in steps:
                    pe.wait_ge(dctx_scaled, s + 1)
                    for t in range(TPS):
                        ins = pe.transpose(B[5][:, t * P:(t + 1) * P], dctx[:, t, :], ident[:])
                    ins.then_inc(dctxT_ready, 1)

            dec_pipeline(pe, dec_turn)
            pe.wait_ge(const_loaded, 16 * N_CONST)
            pe.wait_ge(masks_made, 2)
            pe.wait_ge(w_split, 3 * LAYERS)

            def x_transpose(t, n, first):
                pe.wait_ge(x_staged, n + 1)
                if not first:
                    pe.wait_ge(kT_copied, n - 1)
                pe.transpose(B[5][:, 0:P], x_stage[:, t, :], ident[:]).then_inc(xT_ready, 1)

            def project(l, t, i, ready):
                hi, lo = [w[:, bass.ds(l, 1), i * INNER:(i + 1) * INNER].rearrange("p a f -> p (a f)")
                          for w in (wqkv_hi, wqkv_lo)]
                pe.matmul(B[i], hT_lo[:, t, :], hi, start=True, stop=False)
                pe.matmul(B[i], hT_hi[:, t, :], lo, start=False, stop=False)
                pe.matmul(B[i], hT_hi[:, t, :], hi, start=False, stop=True).then_inc(ready, 1)

            def transposes(bank, src, inc):
                for c in range(NCH):
                    ins = pe.transpose(bank[:, c * P:(c + 1) * P], src[:, c * P:(c + 1) * P], ident[:])
                ins.then_inc(inc, 1)

            def scores(t, n, e):
                pe.wait_ge(qT_copied, n + 1)
                pe.wait_ge(kT_copied, n + 1)
                r = slice(e * DH, (e + 1) * DH)
                S = B[3 + e]
                pe.matmul(S, ident_bf[:], win_mask[t], start=True, stop=False, skip_group_check=True)
                for j in range(4):
                    o = slice(j * P, (j + 1) * P)
                    if t == 0:
                        ins = pe.matmul(S[:, o], qT[r, j, :], kT[r, j, 0:P], start=False, stop=j == 3,
                                        skip_group_check=True)
                    else:
                        pe.matmul(S[0:WIN, o].rearrange("p (w k) -> p w k", w=2), qT[r, j, 0:WIN],
                                  kT[r, j, :].rearrange("p (w k) -> p w k", k=WIN)[:, 2:0:-1, :], start=False,
                                  stop=j == 3, skip_group_check=True)
                        ins = pe.matmul(S[WIN:P, o], qT[r, j, WIN:P], kT[r, j, P:2 * P], start=False, stop=j == 3,
                                        skip_group_check=True)
                ins.then_inc(s_ready, 1)

            def apply_values(t, n, vmid_count):
                pe.wait_ge(v_copied, n + 1)
                if t:
                    pe.wait_ge(vmid_ready, vmid_count)
                for e in range(2):
                    pe.wait_ge((pTe_copied, pTo_copied)[e], n + 1)
                    for j in range(4):
                        h = slice((2 * j + e) * DH, (2 * j + e + 1) * DH)
                        O = B[7][e * DH:(e + 1) * DH, j * P:(j + 1) * P]
                        if t == 0:
                            ins = pe.matmul(O, v_sb[:, 0, h], pT[:, e, j * P:(j + 1) * P], start=True, stop=True)
                        else:
                            pe.matmul(O[:, 0:WIN], v_mid[:, h], pT[:, e, j * P:j * P + WIN], start=True, stop=True)
                            ins = pe.matmul(O[:, WIN:P], v_sb[:, 1, h], pT[:, e, j * P + WIN:(j + 1) * P],
                                            start=True, stop=True)
                ins.then_inc(o_ready, 1)

            def norm_transposes(m):
                pe.wait_ge(hn_ready, m + 1)
                for t in range(TPS):
                    ins = pe.transpose(B[6][:, t * P:(t + 1) * P], hn[:, t, :], ident[:])
                ins.then_inc(hnT_ready, 1)

            def output(l, n):
                pe.wait_ge(oT_copied, n + 1)
                for c in range(NCH):
                    ins = pe.matmul(B[7][:, 0:D], oT[:, c, :],
                                    wo_sb[:, bass.ds(l, 1), c, :].rearrange("p a d -> p (a d)"), start=c == 0,
                                    stop=c == NCH - 1)
                ins.then_inc(y_ready, 1)

            with pe.Fori(0, LAYERS) as l:
                n0 = l * NT
                def turn(s, t, steps):
                    n = n0 + TPS * s + t
                    u = 1 - t
                    if 0 in steps:
                        if 1 in steps:
                            pe.wait_ge(qT_copied, n + 2)
                        pe.wait_ge(pn_ready, 2 * n + 1)
                        transposes(B[6], prob[:, 0, :], pTe_ready)
                        if 1 in steps:
                            pe.wait_ge(v_copied, n + 2)
                        pe.wait_ge(pn_ready, 2 * n + 2)
                        transposes(B[2], prob[:, 1, :], pTo_ready)
                    if 1 in steps and 0 not in steps:
                        pe.wait_ge(seq_done, l * BATCH + BATCH)
                    if 3 in steps:
                        x_transpose(u, n + 3, first=1 not in steps)
                    if 1 in steps:
                        scores(u, n + 1, 0)
                        scores(u, n + 1, 1)
                    if 0 in steps:
                        if 1 in steps:
                            pe.wait_ge(nbias_ready, 2 * n + 3)
                        else:
                            pe.wait_ge(x_done, n)
                        apply_values(t, n, l * BATCH + s + 1)
                    if 0 in steps and 1 not in steps:
                        norm_transposes(l * BATCH)
                    if 3 in steps:
                        if 2 in steps:
                            pe.wait_ge(qab_ready, n + 3)
                        pe.wait_ge(hT_split, n + 4)
                        project(l, u, 0, q_ready)
                    if 2 in steps:
                        if 0 in steps:
                            pe.wait_ge(pTo_copied, n + 1)
                        elif 1 in steps:
                            pe.wait_ge(v_copied, n + 2)
                        project(l, t, 2, v_ready)
                    if 2 in steps and 0 in steps:
                        pe.wait_ge(qrot_ready, n + 3)
                        transposes(B[6], qrot, qT_ready)
                    if 3 in steps:
                        if 2 in steps:
                            pe.wait_ge(kab_ready, n + 3)
                        project(l, u, 1, k_ready)
                    if 2 in steps and 0 not in steps:
                        pe.wait_ge(qrot_ready, n + 3)
                        transposes(B[6], qrot, qT_ready)
                    if 0 in steps:
                        output(l, n)
                    if 2 in steps:
                        pe.wait_ge(krot_ready, n + 3)
                        transposes(B[5], krot, kT_ready)

                pipeline(pe, turn)

                def up(m, parity, j):
                    H = HSIZE[j]
                    hi, lo = hnT_hi[:, parity, :], hnT_lo[:, parity, :]
                    for first, cols in ((HID, slice(SEQ, 2 * SEQ)), (0, slice(0, SEQ))):
                        f = slice(first + j * HC, first + j * HC + H)
                        pe.matmul(B[j][0:H, cols], w1_lo[:, f], hi, start=True, stop=False)
                        pe.matmul(B[j][0:H, cols], w1_hi[:, f], lo, start=False, stop=False)
                        ins = pe.matmul(B[j][0:H, cols], w1_hi[:, f], hi, start=False, stop=True)
                    ins.then_inc(up_ready, 1)

                def down(m, parity, j):
                    H = HSIZE[j]
                    if j == 0:
                        pe.wait_ge(seq_done, BATCH + m)
                    pe.wait_ge(hid_ready, m * NHC + j + 1)
                    for t in range(TPS):
                        ins = pe.matmul(B[3 + t][:, 0:D], hidT[0:H, parity, j, t * P:(t + 1) * P],
                                        w2_sb[0:H, bass.ds(l, 1), j, :].rearrange("p a d -> p (a d)"),
                                        start=j == 0, stop=j == NHC - 1)
                    if j == NHC - 1:
                        ins.then_inc(down_ready, 1)

                def ffn_turn(s, parity, steps):
                    m = l * BATCH + s
                    if 2 in steps:
                        if 1 in steps:
                            pe.wait_ge(hnT_copied, m + 2)
                        norm_transposes(m + 2)
                    if 1 in steps:
                        if 0 not in steps:
                            pe.wait_ge(w1_split, l + 1)
                        pe.wait_ge(hnT_split, m + 2)
                    for j in range(NHC):
                        if 0 in steps:
                            pe.wait_ge(hid_ready, m * NHC + j + 1)
                        if 1 in steps:
                            up(m + 1, 1 - parity, j)
                        if 0 in steps:
                            down(m, parity, j)

                ffn_pipeline(pe, ffn_turn, begin=-1)


def constants():
    a, b = np.arange(WIN)[:, None], np.arange(WIN)[None, :]
    causal, band, none = b <= a, b >= a, np.zeros((WIN, WIN), bool)
    first = np.block([[causal, none], [band, causal]])
    second = np.block([[causal, band], [band, causal]])
    i, j = np.arange(SEQ)[:, None], np.arange(SEQ)[None, :]
    dec = j < i
    dec[0, 0] = True
    seen = np.concatenate([first] * 4 + [second] * 4 + [dec[:P, :P], dec[P:, :]], axis=1)
    masks = np.where(seen, 0.0, MASKED).astype(np.float32)

    half_idx = np.arange(0, DH, 2, dtype=np.float32)
    inv_freq = (np.float32(1.0) / np.float32(10000.0) ** (half_idx / np.float32(DH))).astype(np.float32)
    tok = np.arange(SEQ, dtype=np.float32)
    freqs = tok[:, None] * inv_freq[None, :]
    freqs = np.concatenate([freqs, freqs], axis=-1)
    base = (half_idx + np.float32(0.4 * DH)) / np.float32(1.4 * DH)
    power = (tok - SEQ // 2) / np.float32(WIN // 2)
    scale = base[None, :] ** power[:, None]
    scale = np.concatenate([scale, scale], axis=-1)
    sign = np.where(np.arange(DH) < DH // 2, -1.0, 1.0).astype(np.float32)
    cos, sin = np.cos(freqs), np.sin(freqs) * sign
    tables = np.stack([QK_SCALE * cos * scale, QK_SCALE * sin * scale, cos / scale, sin / scale])
    rope = tables.reshape(4, TPS, P, DH).transpose(2, 0, 1, 3)
    return (np.ascontiguousarray(rope, dtype=np.float32), np.ascontiguousarray(masks),
            np.eye(P, dtype=np.float32))


def kernel(**inputs):
    import concourse.bacc as bacc
    from concourse.bass_utils import run_bass_kernel_spmd

    g = {k: np.asarray(v) for k, v in inputs.items()}
    w2 = np.zeros((LAYERS, NHC * HC, D), np.float32)
    w2[:, :HID] = g["L0_ffn_w2"]
    b1 = np.zeros((LAYERS, 2, NHC * HC), np.float32)
    b1[:, :, :HID] = g["L0_ffn_b1"].reshape(LAYERS, 2, HID)
    q_s, k_s = g["L0_ffn_q_scale"], g["L0_ffn_k_scale"]
    rope, masks, identity = constants()
    arrays = {
        "x": g["L0_attn_hidden_states"].reshape(BATCH * SEQ, D),
        "w_dec": g["L0_attn_w_dec_attn"],
        "w_outT": g["L0_attn_w_out"].T.reshape(2, D, D).transpose(1, 0, 2),
        "b_out": g["L0_attn_b_out"],
        "wqkv": g["L0_ffn_wqkv"],
        "qk_scale": np.stack([q_s, np.roll(q_s, DH // 2, -1), k_s, np.roll(k_s, DH // 2, -1)], axis=1),
        "wo": g["L0_ffn_wo"].reshape(LAYERS, NCH, P, D).transpose(0, 2, 1, 3),
        "ln_gb": np.stack([g["L0_ffn_ln_g"], g["L0_ffn_ln_b"]], axis=-1).transpose(1, 0, 2),
        "w1": g["L0_ffn_w1"],
        "b1": b1.reshape(LAYERS, 2 * NHC, HC).transpose(2, 0, 1),
        "w2": w2.reshape(LAYERS, NHC, HC, D).transpose(2, 0, 1, 3),
        "b2": g["L0_ffn_b2"],
        "rope": rope,
        "masks": masks,
        "identity": identity,
    }
    arrays = {f"in_{k}": np.ascontiguousarray(v) for k, v in arrays.items()}
    nc = bacc.Bacc("TRN2", target_bir_lowering=False, num_devices=1)
    aps = [nc.dram_tensor(k, v.shape, mybir.dt.from_np(v.dtype), kind="ExternalInput").ap() for k, v in arrays.items()]
    out = nc.dram_tensor("out", (BATCH * SEQ, D), F32, kind="ExternalOutput").ap()
    program(nc, *aps, out)
    r = run_bass_kernel_spmd(nc, [arrays], core_ids=[0])
    return r.results[0]["out"].reshape(BATCH, SEQ, D)
```
